# Optimizing a Trainium2 kernel written in Bass

```python
import numpy as np
import jax
import jax.numpy as jnp

def _softmax(x, axis=-1):
    return jax.nn.softmax(x, axis=axis)

def _gelu(x):
    return jax.nn.gelu(x, approximate=True)

def _silu(x):
    return jax.nn.silu(x)

def _sigmoid(x):
    return jax.nn.sigmoid(x)

def _layernorm(x, axis=-1, eps=1e-05):
    m = jnp.mean(x, axis=axis, keepdims=True)
    v = jnp.var(x, axis=axis, keepdims=True)
    return (x - m) / jnp.sqrt(v + eps)

def _scatter_add(tgt, idx, src, axis=0):
    return tgt.at[idx].add(src)

def _segment_sum(src, seg, n):
    return jax.ops.segment_sum(src, seg, n)
kernel_name = 'mk_metaformer_d2_conv_nhwc128_r2_8fa203'

def setup_inputs(seed: int=0):
    np.random.seed(seed)
    _w = jnp.asarray

    def _rec_inputs():
        import jax
        import jax.numpy as jnp
        _gk = jax.random.key(seed)
        x = -0.000125 + 0.9999 * jax.random.normal(jax.random.fold_in(_gk, 1), (16, 64, 64, 64), jnp.float32)
        return x
    x = _rec_inputs()

    def _L0_conv_setup():
        import jax, jax.numpy as jnp
        import numpy as np
        N, L, D = (16, 64, 64)
        H, C = (8, 16)
        EPS = 1e-05
        key = jax.random.key(seed)
        ks = jax.random.split(key, 10)
        s = 0.02
        return {'z': jax.random.normal(ks[0], (N, L, L, D), dtype=jnp.float32), 'ln_w': jnp.ones((D,), jnp.float32), 'ln_b': jnp.zeros((D,), jnp.float32), 'Wq': jax.random.normal(ks[1], (D, H * C), jnp.float32) * s, 'Wk': jax.random.normal(ks[2], (D, H * C), jnp.float32) * s, 'Wv': jax.random.normal(ks[3], (D, H * C), jnp.float32) * s, 'Wg': jax.random.normal(ks[4], (D, H * C), jnp.float32) * s, 'bg': jnp.zeros((H * C,), jnp.float32), 'Wo': jax.random.normal(ks[5], (H * C, D), jnp.float32) * s, 'bo': jnp.zeros((D,), jnp.float32)}
    _L0_conv_all = _L0_conv_setup()
    _L0_conv_in = {k: v for k, v in _L0_conv_all.items() if k in ('ln_w', 'ln_b', 'Wq', 'Wk', 'Wv', 'Wg', 'bg', 'Wo', 'bo')}
    del _L0_conv_all

    def _L0_ffn_setup():
        import jax, jax.numpy as jnp
        import numpy as np
        B, N, D, C, E, K = (8, 4096, 64, 64, 8, 2)
        key = jax.random.key(seed)
        k0, k1, k2 = jax.random.split(key, 3)
        x = jax.random.normal(k0, (B, N, D), dtype=jnp.float32)
        router_w = jax.random.normal(k1, (D, E), dtype=jnp.float32) * 0.05
        router_b = jnp.zeros((E,), dtype=jnp.float32)
        expert_w = jax.random.normal(k2, (E, D, C), dtype=jnp.float32) * (1.0 / np.sqrt(D))
        expert_b = jnp.zeros((E, C), dtype=jnp.float32)
        return {'x': x, 'router_w': router_w, 'router_b': router_b, 'expert_w': expert_w, 'expert_b': expert_b}
    _L0_ffn_all = _L0_ffn_setup()
    _L0_ffn_in = {k: v for k, v in _L0_ffn_all.items() if k in ('router_w', 'router_b', 'expert_w', 'expert_b')}
    del _L0_ffn_all

    def _L1_conv_setup():
        import jax, jax.numpy as jnp
        import numpy as np
        from jax import lax
        H = 64

        def _ema_scan(x):
            xt = jnp.moveaxis(x, 1, 0)

            def step(s, xi):
                s = s * 0.9 + xi * 0.1
                return (s, s)
            _, ys = lax.scan(step, jnp.zeros_like(xt[0]), xt)
            return jnp.moveaxis(ys, 0, 1)
        key = jax.random.key(seed)
        k1, k2, k3, k4, k5 = jax.random.split(key, 5)
        B, T, N = (4, 48, 256)
        x = jax.random.normal(k1, (B, T, N, H), dtype=jnp.float32)
        s = 1.0 / np.sqrt(H)
        W_exp = jax.random.uniform(k2, (2 * H, H), jnp.float32, -s, s)
        b_exp = jax.random.uniform(k3, (2 * H,), jnp.float32, -s, s)
        W_con = jax.random.uniform(k4, (H, H), jnp.float32, -s, s)
        b_con = jax.random.uniform(k5, (H,), jnp.float32, -s, s)
        return {'spatial_temporal_representation': x, 'W_exp': W_exp, 'b_exp': b_exp, 'W_con': W_con, 'b_con': b_con}
    _L1_conv_all = _L1_conv_setup()
    _L1_conv_in = {k: v for k, v in _L1_conv_all.items() if k in ('W_exp', 'b_exp', 'W_con', 'b_con')}
    del _L1_conv_all

    def _L1_ffn_setup():
        import jax, jax.numpy as jnp
        import numpy as np
        B, S, D, E, H, O, K = (256, 1024, 64, 32, 256, 64, 8)
        key = jax.random.key(seed)
        k0, k1, k2, k3 = jax.random.split(key, 4)
        x = jax.random.normal(k0, (B, S, D), dtype=jnp.float32)
        gate_w = jax.random.normal(k1, (E, D), dtype=jnp.float32) * (1.0 / np.sqrt(D))
        gate_b = jnp.zeros((E,), dtype=jnp.float32)
        weight1 = jax.random.uniform(k2, (E, D + 1, H), dtype=jnp.float32, minval=-1.0, maxval=1.0) * (1.0 / np.sqrt(D + 1))
        weight2 = jax.random.uniform(k3, (E, H + 1, O), dtype=jnp.float32, minval=-1.0, maxval=1.0) * (1.0 / np.sqrt(H + 1))
        return {'x': x, 'gate_w': gate_w, 'gate_b': gate_b, 'weight1': weight1, 'weight2': weight2}
    _L1_ffn_all = _L1_ffn_setup()
    _L1_ffn_in = {k: v for k, v in _L1_ffn_all.items() if k in ('gate_w', 'gate_b', 'weight1', 'weight2')}
    del _L1_ffn_all
    return {'x': x, 'L0_conv_ln_w': _L0_conv_in['ln_w'], 'L0_conv_ln_b': _L0_conv_in['ln_b'], 'L0_conv_Wq': _L0_conv_in['Wq'], 'L0_conv_Wk': _L0_conv_in['Wk'], 'L0_conv_Wv': _L0_conv_in['Wv'], 'L0_conv_Wg': _L0_conv_in['Wg'], 'L0_conv_bg': _L0_conv_in['bg'], 'L0_conv_Wo': _L0_conv_in['Wo'], 'L0_conv_bo': _L0_conv_in['bo'], 'L0_ffn_router_w': _L0_ffn_in['router_w'], 'L0_ffn_router_b': _L0_ffn_in['router_b'], 'L0_ffn_expert_w': _L0_ffn_in['expert_w'], 'L0_ffn_expert_b': _L0_ffn_in['expert_b'], 'L1_conv_W_exp': _L1_conv_in['W_exp'], 'L1_conv_b_exp': _L1_conv_in['b_exp'], 'L1_conv_W_con': _L1_conv_in['W_con'], 'L1_conv_b_con': _L1_conv_in['b_con'], 'L1_ffn_gate_w': _L1_ffn_in['gate_w'], 'L1_ffn_gate_b': _L1_ffn_in['gate_b'], 'L1_ffn_weight1': _L1_ffn_in['weight1'], 'L1_ffn_weight2': _L1_ffn_in['weight2']}

def reference(x, L0_conv_ln_w, L0_conv_ln_b, L0_conv_Wq, L0_conv_Wk, L0_conv_Wv, L0_conv_Wg, L0_conv_bg, L0_conv_Wo, L0_conv_bo, L0_ffn_router_w, L0_ffn_router_b, L0_ffn_expert_w, L0_ffn_expert_b, L1_conv_W_exp, L1_conv_b_exp, L1_conv_W_con, L1_conv_b_con, L1_ffn_gate_w, L1_ffn_gate_b, L1_ffn_weight1, L1_ffn_weight2):
    import jax
    import jax.numpy as jnp

    def _L0_conv_ref(z, ln_w, ln_b, Wq, Wk, Wv, Wg, bg, Wo, bo):
        import jax, jax.numpy as jnp
        import numpy as np
        N, L, D = (16, 64, 64)
        H, C = (8, 16)
        EPS = 1e-05
        n, l, _, d = z.shape
        mu = jnp.mean(z, axis=-1, keepdims=True)
        var = jnp.var(z, axis=-1, keepdims=True)
        zn = (z - mu) * jax.lax.rsqrt(var + EPS) * ln_w + ln_b
        q = (zn @ Wq).reshape(n, l, l, H, C)
        k = (zn @ Wk).reshape(n, l, l, H, C)
        v = (zn @ Wv).reshape(n, l, l, H, C)
        g = jax.nn.sigmoid(zn @ Wg + bg).reshape(n, l, l, H, C)
        att = jnp.einsum('iabhc,jabhc->ijabh', q, k) * (1.0 / np.sqrt(C))
        att = jax.nn.softmax(att, axis=1)
        o = jnp.einsum('ijabh,jabhc->iabhc', att, v) * g
        out = o.reshape(n, l, l, H * C) @ Wo + bo
        return out

    def _L0_ffn_ref(x, router_w, router_b, expert_w, expert_b):
        import jax, jax.numpy as jnp
        import numpy as np
        B, N, D, C, E, K = (8, 4096, 64, 64, 8, 2)
        router_probs = jax.nn.softmax(x @ router_w + router_b, axis=-1)
        top_p, top_i = jax.lax.top_k(router_probs, K)
        top_p = top_p / jnp.sum(top_p, axis=-1, keepdims=True)
        expert_out = jnp.einsum('bnd,edc->bnec', x, expert_w) + expert_b
        gathered = jnp.take_along_axis(expert_out, top_i[..., None], axis=2)
        return jnp.einsum('bnk,bnkc->bnc', top_p, gathered)

    def _L1_conv_ref(spatial_temporal_representation, W_exp, b_exp, W_con, b_con):
        import jax, jax.numpy as jnp
        import numpy as np
        from jax import lax
        H = 64

        def _ema_scan(x):
            xt = jnp.moveaxis(x, 1, 0)

            def step(s, xi):
                s = s * 0.9 + xi * 0.1
                return (s, s)
            _, ys = lax.scan(step, jnp.zeros_like(xt[0]), xt)
            return jnp.moveaxis(ys, 0, 1)
        x = spatial_temporal_representation
        expanded = jnp.einsum('btnh,oh->btno', x, W_exp) + b_exp
        state_primary, state_gating = jnp.split(expanded, 2, axis=-1)
        gated_activation = jax.nn.sigmoid(_ema_scan(state_gating))
        out = jnp.einsum('btnh,oh->btno', state_primary * gated_activation, W_con) + b_con
        return out

    def _L1_ffn_ref(x, gate_w, gate_b, weight1, weight2):
        import jax, jax.numpy as jnp
        import numpy as np
        B, S, D, E, H, O, K = (256, 1024, 64, 32, 256, 64, 8)
        Bn, Sn, Dn = x.shape
        logits = jnp.einsum('bsd,ed->bse', x, gate_w) + gate_b
        probs = jax.nn.softmax(logits, axis=1)
        vals, idx = jax.lax.top_k(probs.transpose(0, 2, 1), K)
        topv = vals.transpose(0, 2, 1)
        topi = idx.transpose(0, 2, 1)
        flat_idx = topi.reshape(Bn, K * E)
        gathered = jnp.take_along_axis(x, flat_idx[:, :, None], axis=1)
        gathered = gathered.reshape(Bn, K, E, Dn)
        pooled = jnp.einsum('bked,bke->bed', gathered, topv)
        ones = jnp.ones((E, Bn, 1), dtype=x.dtype)
        h = jnp.concatenate([pooled.transpose(1, 0, 2), ones], axis=-1)
        h = jax.nn.gelu(jnp.einsum('ebd,edh->ebh', h, weight1), approximate=False)
        h = jnp.concatenate([h, ones], axis=-1)
        out = jnp.einsum('ebh,eho->ebo', h, weight2)
        out = out.transpose(1, 0, 2)
        weighted = jnp.einsum('beo,bke->bkeo', out, topv).reshape(Bn, K * E, O)
        outputs = jnp.zeros((Bn, Sn, O), dtype=x.dtype)
        outputs = outputs.at[jnp.arange(Bn)[:, None], flat_idx].add(weighted)
        return outputs

    def _gn(v, G=32, eps=1e-05):
        B_, H_, W_, C_ = v.shape
        g = v.reshape(B_, H_, W_, G, C_ // G)
        m = jnp.mean(g, axis=(1, 2, 4), keepdims=True)
        s = jnp.var(g, axis=(1, 2, 4), keepdims=True)
        return ((g - m) / jnp.sqrt(s + eps)).reshape(v.shape)

    def _ln_c(v, eps=1e-06):
        m = jnp.mean(v, axis=-1, keepdims=True)
        s = jnp.var(v, axis=-1, keepdims=True)
        return (v - m) / jnp.sqrt(s + eps)

    def _ln_t(v, eps=1e-05):
        m = jnp.mean(v, axis=-1, keepdims=True)
        s = jnp.var(v, axis=-1, keepdims=True)
        return (v - m) / jnp.sqrt(s + eps)

    def _to_tokens(v):
        B_, H_, W_, C_ = v.shape
        return v.reshape(B_, H_ * W_, C_)

    def _from_tokens(t, like):
        return t.reshape(like.shape)
    x = x + _L0_conv_ref(_ln_c(x), L0_conv_ln_w, L0_conv_ln_b, L0_conv_Wq, L0_conv_Wk, L0_conv_Wv, L0_conv_Wg, L0_conv_bg, L0_conv_Wo, L0_conv_bo)
    t = _to_tokens(x)
    t = t + _L0_ffn_ref(_ln_t(t), L0_ffn_router_w, L0_ffn_router_b, L0_ffn_expert_w, L0_ffn_expert_b)
    x = _from_tokens(t, x)
    x = x + _L1_conv_ref(_ln_c(x), L1_conv_W_exp, L1_conv_b_exp, L1_conv_W_con, L1_conv_b_con)
    t = _to_tokens(x)
    t = t + _L1_ffn_ref(_ln_t(t), L1_ffn_gate_w, L1_ffn_gate_b, L1_ffn_weight1, L1_ffn_weight2)
    x = _from_tokens(t, x)
    return x

_drawn_inputs = setup_inputs


def setup_inputs(seed=0):
    import zlib

    import numpy as np

    out = dict(_drawn_inputs(seed))
    spreads = {'L0_conv_ln_w': (1.0, 0.6),
     'L0_conv_ln_b': (0.0, 0.316),
     'L0_conv_bg': (0.0, 0.8),
     'L0_conv_bo': (0.0, 0.1),
     'L0_ffn_router_b': (0.0, 0.1),
     'L0_ffn_expert_b': (0.0, 0.1),
     'L1_ffn_gate_b': (0.0, 0.1)}
    factors = {'L0_conv_Wq': 8.0,
     'L0_conv_Wk': 8.0,
     'L0_conv_Wg': 5.656,
     'L1_conv_b_exp': 2.968,
     'L1_ffn_gate_w': 8.0,
     'L1_ffn_weight1': 8.0,
     'L1_ffn_weight2': 8.0}
    for name, (base, spread) in spreads.items():
        noise = np.random.default_rng([zlib.crc32(name.encode()), seed]).standard_normal(out[name].shape)
        drawn = base * np.exp(spread * noise) if base else spread * noise
        out[name] = jnp.asarray(drawn.astype(out[name].dtype))
    for name, factor in factors.items():
        out[name] = (out[name] * factor).astype(out[name].dtype)
    return out
```

```python
from contextlib import ExitStack

import concourse.bass as bass
from concourse import mybir

ALU = mybir.AluOpType
ACT = mybir.ActivationFunctionType
AX = mybir.AxisListType
F32 = mybir.dt.float32
BF16 = mybir.dt.bfloat16

P = 128
QT = 4
QTOK = QT * P
BIG = 1e30

TURNS = ["scan_out", "ffn_t", "route", "att_t", "k", "q", "gate", "v", "gates_t",
         "spread0", "spread1", "spread2", "spread3", "expert", "pick_t", "pick",
         "att_out", "conv_t", "expand"]
BEHIND = {"att_t": 0, "k": 0, "q": 0, "gate": 0, "v": 0, "att_out": 0,
          "ffn_t": 1, "route": 1, "gates_t": 1, "spread0": 1, "spread1": 1, "spread2": 1,
          "spread3": 1, "expert": 1, "conv_t": 1, "expand": 1,
          "scan_out": 2, "pick_t": 2, "pick": 2}


def build(nc, x, ln_w, ln_b, Wq, Wk, Wv, Wg, bg, Wo, bo, router_w, router_b, expert_w, expert_b,
          W_exp, b_exp, W_con, b_con, gate_w, gate_b, weight1, weight2, out):
    N, A, B, D = x.shape
    HC = Wq.shape[1]
    H = 8
    C = HC // H
    NE = router_w.shape[1]
    EP, HID = gate_w.shape[0], weight1.shape[2]
    TOK = A * B
    NG = N // 4
    IT = TOK // P
    assert HC == P and N == 16 and D == 64 and A == 64 and B == 64 and EP == 32

    x_cols = x.rearrange("n (q t p) b d -> p q b n t d", q=2, t=QT)
    x3_dram = nc.dram_tensor("x3_scratch", [N, A, B, D], F32).ap()
    x3_cols = x3_dram.rearrange("n (q t p) b d -> p q b n t d", q=2, t=QT)
    x3_imgs = x3_dram.rearrange("n a b d -> n (a b d)").rearrange("n (p f) -> n p f", p=P)
    out_imgs = out.rearrange("n a b d -> n (a b d)").rearrange("n (p f) -> n p f", p=P)

    with ExitStack() as ctx:
        def sb(name, shape, dt=F32, c=ctx):
            return c.enter_context(nc.sbuf_tensor(name, shape, dt))

        def pair(name, shape, dt=F32, c=ctx):
            return [sb(f"{name}{q}", shape, dt, c) for q in range(2)]

        def sem(name):
            return ctx.enter_context(nc.semaphore(name))

        ident = sb("ident", [P, P])
        picks = sb("picks", [P, NG, TOK])
        banks = [ctx.enter_context(nc.psum_tensor(f"bank{i}", [P, 512], F32)) for i in range(8)]
        shared, s_bank, o_bank = banks[0:2], banks[2:4], banks[4:8]

        with ExitStack() as cols:
            def cb(name, shape, dt=F32):
                return sb(name, shape, dt, cols)

            def cpair(name, shape, dt=F32):
                return pair(name, shape, dt, cols)

            ident_bf = cb("ident_bf", [P, P], BF16)
            lnw_col, lnb_col, bg_col = cb("lnw_col", [D, 1]), cb("lnb_col", [D, 1]), cb("bg_col", [P, 1])
            w_qkgv = cb("w_qkgv", [D, 4, HC])
            w_o = cb("w_o", [P, D])
            bo_rows, bcon_rows, rb_rows = cb("bo_rows", [P, D]), cb("bcon_rows", [P, D]), cb("rb_rows", [P, NE])
            w_router = cb("w_router", [D, NE])
            w_expert = cb("w_expert", [P, NE // 2, D])
            b_expert = cb("b_expert", [32, D])
            b_expert_bf = cb("b_expert_bf", [32, 3, D], BF16)
            b_rest = cb("b_rest", [32, D])
            wexp_raw, wcon_raw, gw_raw = cb("wexp_raw", [2 * D, D]), cb("wcon_raw", [D, 2, D]), cb("gw_raw", [EP, D])
            w_expand = cb("w_expand", [D, 2 * D])
            w_con = cb("w_con", [P, D])
            w_pick = cb("w_pick", [D, EP])
            bprim_col, bgate_col, gb_col = cb("bprim_col", [P, 1]), cb("bgate_col", [P, 1]), cb("gb_col", [P, 1])
            block_of = cb("block_of", [P, 8])
            head_of = cb("head_of", [P, 4])
            odd_even = cb("odd_even", [P, 2])
            other_big = cb("other_big", [P, 2])
            spread_sel3 = cb("spread_sel3", [32, 3, 8])
            spread_sel8 = cb("spread_sel8", [32, 8])
            spread_sel = cb("spread_sel", [32, NE // 2, 2, D], BF16)
            decay = cb("decay", [P, 8, A])
            first_wins = cb("first_wins", [P, NE])
            minus_half = cb("minus_half", [P, QT])

            x_in = cpair("x_in", [P, QT, D])
            x_bo = cpair("x_bo", [P, QT, D])
            x1 = cpair("x1", [P, QT, D])
            x2 = cpair("x2", [P, QT, D])
            x2_bc = cpair("x2_bc", [P, QT, D])
            x3 = cpair("x3", [P, QT, D])
            norm = {k: cpair(f"norm_{k}", [P, QT, D]) for k in ("att", "ffn", "conv", "pick")}
            norm_twice = cpair("norm_twice", [P, QT, 2, D])
            bn = {k: cpair(f"bn_{k}", [P, QT, 6]) for k in norm}
            mv = {k: cpair(f"mv_{k}", [P, QT, 2]) for k in norm}
            rstd = {k: cpair(f"rstd_{k}", [P, 2, QT]) for k in norm}
            zT = cpair("zT", [D, QTOK])
            qT = cpair("qT", [P, QTOK])
            kT = cpair("kT", [P, 4, QTOK])
            gT = cpair("gT", [P, QTOK])
            v_sb = cpair("v_sb", [P, QT, HC])
            probs = cb("probs", [P, 32, 2, 16])
            probsT = cb("probsT", [P, 32, 32])
            smax = cb("smax", [P, 32, 2])
            ssum = cb("ssum", [P, 32])
            o_half = cb("o_half", [P, 2, 4, QT, 32])
            oT = cb("oT", [P, QTOK])
            ogT = cb("ogT", [P, QTOK])
            tT = cpair("tT", [P, QTOK])
            lg = cb("lg", [P, QT, NE])
            pick1, pick2 = cb("pick1", [P, QT, NE]), cb("pick2", [P, QT, NE])
            lg2, eq = cb("lg2", [P, QT, NE]), cb("eq", [P, QT, NE])
            m1, m2, mw = cb("m1", [P, QT]), cb("m2", [P, QT]), cb("mw", [P, QT])
            g2e, g1v, g2v, gden = cb("g2e", [P, QT]), cb("g1v", [P, QT]), cb("g2v", [P, QT]), cb("gden", [P, QT])
            gates = cb("gates", [P, QT, NE])
            gates_rest = cb("gates_rest", [P, QT, NE])
            gates_bf = cb("gates_bf", [P, QT, 4, NE], BF16)
            gatesT = cb("gatesT", [32, QTOK], BF16)
            xg = cb("xg", [P, NE // 2, QTOK])
            cT = cb("cT", [D, QTOK])
            prim, gpre = cb("prim", [P, 8, A]), cb("gpre", [P, 8, A])
            ema, ema_t = cb("ema", [P, 8, A]), cb("ema_t", [P, 8, A])
            gated = cpair("gated", [P, A // 2, N])
            lT = cb("lT", [D, QTOK])

            s_weights, s_pool_setup, s_dve_setup, s_wT = sem("weights_loaded"), sem("pool_setup"), sem("dve_setup"), sem("weights_transposed")
            s_act_setup = sem("act_setup")
            filled = {k: sem(f"filled_{k}") for k in TURNS}
            drained = {k: sem(f"drained_{k}") for k in TURNS}
            s_x = [sem(f"x_loaded{q}") for q in range(2)]
            s_bo = sem("x_bo_done")
            s_bn = {k: sem(f"stats_{k}") for k in norm}
            s_agg = {k: sem(f"aggregated_{k}") for k in norm}
            s_norm = {k: sem(f"normalized_{k}") for k in norm}
            s_pn = {k: sem(f"pool_norm_{k}") for k in norm}
            s_scores, s_sub, s_exp, s_rden, s_probs, s_probsT = (sem("scores_filled"), sem("scores_read"), sem("exp_done"),
                                                                 sem("denominators"), sem("probs_normalized"), sem("probs_transposed"))
            s_smax_chain, s_o, s_o_read, s_o_sum, s_og = sem("softmax_chain"), sem("o_filled"), sem("o_read"), sem("o_summed"), sem("o_gated")
            s_top, s_diff, s_ratio, s_gates, s_gsplit = sem("top_chain"), sem("top_diff"), sem("top_ratio"), sem("gates_done"), sem("gates_split")
            s_gchain = sem("gates_chain")
            s_x2bc = sem("x2_bc_done")
            s_ema, s_emat, s_gated = sem("ema_done"), sem("ema_tanh"), sem("gated_done")
            s_x3_store = [sem(f"x3_stored{q}") for q in range(2)]

            N_LOADS = 30
            N_POOL_SETUP = 20

            def at(i, kind_behind, q, n=1, more=0):
                return (i - kind_behind) * (2 * n) + ((q + 1) * n + more)

            def wait(eng, s, value):
                if not isinstance(value, int) or value > 0:
                    eng.wait_ge(s, value)

            def wait_apart(eng, s, value):
                if isinstance(value, int):
                    return wait(eng, s, value)
                held = eng.to_reg(value)
                plain(eng)
                eng.wait_ge(s, held)

            def plain(eng):
                eng.wait_ge(s_pool_setup, N_POOL_SETUP)

            def runs(i, behind):
                return not isinstance(i, int) or 0 <= i - behind < B

            def bank_of(q, name):
                return (len(TURNS) * q + TURNS.index(name)) % 2

            def bank_free(pe, i, q, name):
                pos = len(TURNS) * q + TURNS.index(name)
                back = pos - 2
                for _ in range(3 * len(TURNS)):
                    cols_back = 0
                    p = back
                    while p < 0:
                        p += 2 * len(TURNS)
                        cols_back += 1
                    prev, pq = TURNS[p % len(TURNS)], p // len(TURNS)
                    if not isinstance(i, int):
                        return pe.wait_ge(drained[prev], at(i, cols_back + BEHIND[prev], pq))
                    if i - cols_back < 0:
                        return None
                    if runs(i - cols_back, BEHIND[prev]):
                        return pe.wait_ge(drained[prev], at(i, cols_back + BEHIND[prev], pq))
                    back -= 2

            class Chain:

                def __init__(self, eng, s, per, i, behind, q):
                    self.eng, self.s, self.per, self.n = eng, s, per, 0
                    self.base = at(i, behind, q, per) - per

                def link(self, ins):
                    self.n += 1
                    ins.then_inc(self.s, 1)

                def join(self):
                    self.eng.wait_ge(self.s, self.base + self.n)

                def end(self):
                    assert self.n == self.per, (self.n, self.per)

            def columns(engine, step):
                for i in range(3):
                    step(i)
                with engine.Fori(3, B) as i:
                    step(i)
                for i in range(B, B + 2):
                    step(i)

            block = cols.enter_context(nc.Block())

            @block.sync
            def _(sp):
                loads = [(lnw_col[:], ln_w.unsqueeze(1)), (lnb_col[:], ln_b.unsqueeze(1)), (bg_col[:], bg.unsqueeze(1)),
                         (w_qkgv[:, 0, :], Wq), (w_qkgv[:, 1, :], Wk), (w_qkgv[:, 2, :], Wg), (w_qkgv[:, 3, :], Wv),
                         (w_o[:], Wo), (w_router[:], router_w),
                         (bo_rows[:], bo.unsqueeze(0).broadcast_to([P, D])),
                         (bcon_rows[:], b_con.unsqueeze(0).broadcast_to([P, D])),
                         (rb_rows[:], router_b.unsqueeze(0).broadcast_to([P, NE])),
                         (gw_raw[:], gate_w)]
                we = expert_w.rearrange("(j two) d c -> two d j c", two=2)
                loads += [(w_expert[e * D:(e + 1) * D], we[e]) for e in range(2)]
                loads += [(b_expert[k * NE:(k + 1) * NE], expert_b) for k in range(4)]
                be = b_exp.rearrange("(h d) -> h d", h=2).unsqueeze(2)
                loads += [(bprim_col[k * D:(k + 1) * D], be[0]) for k in range(2)]
                loads += [(bgate_col[k * D:(k + 1) * D], be[1]) for k in range(2)]
                loads += [(gb_col[k * EP:(k + 1) * EP], gate_b.unsqueeze(1)) for k in range(4)]
                for dst, src in loads:
                    sp.dma_start(dst, src).then_inc(s_weights, 16)
                assert len(loads) + 3 == N_LOADS, len(loads)

                def step(i):
                    for q in range(2):
                        if runs(i, 0):
                            wait(sp, s_bo, at(i, 1, q))
                            wait(sp, s_norm["att"], at(i, 1, q))
                            for p in range(8):
                                sp.dma_start(x_in[q][p * N:(p + 1) * N], x_cols[p, q, i]).then_inc(s_x[q], 16)
                        if runs(i, 2):
                            sp.wait_ge(drained["scan_out"], at(i, 2, q))
                            for p in range(8):
                                sp.dma_start(x3_cols[p, q, i - 2], x3[q][p * N:(p + 1) * N]).then_inc(s_x3_store[q], 16)

                columns(sp, step)
                for q in range(2):
                    sp.wait_ge(s_x3_store[q], B * 8 * 16)

            @block.gpsimd
            def _(pool):
                g = nc.gpsimd
                n_setup = [0]

                def setup(ins, wait_for=False):
                    n_setup[0] += 1
                    ins.then_inc(s_pool_setup, 1)
                    if wait_for:
                        pool.wait_ge(s_pool_setup, n_setup[0])

                setup(g.memset(ident[:], 0.0), True)
                setup(g.affine_select(out=ident[:], in_=ident[:], compare_op=ALU.not_equal, fill=1.0, base=0,
                                      pattern=[[-1, P]], channel_multiplier=1), True)
                setup(g.tensor_copy(ident_bf[:], ident[:]))
                setup(g.memset(block_of[:], 1.0), True)
                setup(g.affine_select(out=block_of[:], in_=block_of[:], compare_op=ALU.is_ge, fill=0.0, base=0,
                                      pattern=[[-16, 8]], channel_multiplier=1), True)
                setup(g.affine_select(out=block_of[:], in_=block_of[:], compare_op=ALU.is_ge, fill=0.0, base=15,
                                      pattern=[[16, 8]], channel_multiplier=-1))
                setup(g.memset(spread_sel3[:], 0.0), True)
                setup(g.affine_select(out=spread_sel3[:], in_=spread_sel3[:], compare_op=ALU.not_equal, fill=1.0, base=0,
                                      pattern=[[-8, 3], [-1, 8]], channel_multiplier=1))
                setup(g.memset(decay[:], 0.9), True)
                setup(g.memset(decay[:, :, 0:1], 0.0))
                for e in range(NE):
                    setup(g.memset(first_wins[:, e:e + 1], float(NE - e)))
                setup(g.memset(minus_half[:], -0.5))
                setup(g.memset(gates_bf[:], 0.0), True)
                assert n_setup[0] == N_POOL_SETUP, n_setup[0]
                pool.wait_ge(s_weights, 16 * N_LOADS)
                pool.wait_ge(s_dve_setup, 1)

                def normalize(kind, src, eps_scale, eps_add, i, behind, q):
                    r = rstd[kind][q]
                    ch = Chain(pool, s_pn[kind], 3, i, behind, q)
                    pool.wait_ge(s_agg[kind], at(i, behind, q))
                    wait(pool, filled[{"att": "att_t", "ffn": "ffn_t", "conv": "conv_t", "pick": "pick_t"}[kind]],
                         at(i, behind + 1, q))
                    ch.link(g.tensor_tensor(norm[kind][q][:], src[:],
                                            mv[kind][q][:, :, 0:1].broadcast_to([P, QT, D]), ALU.subtract))
                    ch.link(g.tensor_scalar(r[:, 0, :], mv[kind][q][:, :, 1], eps_scale, eps_add, ALU.mult, ALU.add))
                    ch.join()
                    ch.link(g.tensor_tensor(r[:, 1, :], r[:, 0, :], minus_half[:], ALU.pow))
                    ch.join()
                    ch.end()
                    if kind == "ffn":
                        g.tensor_tensor(norm_twice[q][:], norm[kind][q][:].unsqueeze(2).broadcast_to([P, QT, 2, D]),
                                        r[:, 1, :].unsqueeze(2).unsqueeze(3).broadcast_to([P, QT, 2, D]),
                                        ALU.mult).then_inc(s_norm[kind], 1)
                        return
                    g.tensor_tensor(norm[kind][q][:], norm[kind][q][:],
                                    r[:, 1, :].unsqueeze(2).broadcast_to([P, QT, D]), ALU.mult).then_inc(s_norm[kind], 1)

                def step(i):
                    for q in range(2):
                        if runs(i, 0):
                            normalize("att", x_in[q], 1.0 + 1e-5, 1e-6 * 1e-5, i, 0, q)
                            wait(pool, drained["att_out"], at(i, 1, q))
                            g.tensor_tensor(x_bo[q][:], x_in[q][:], bo_rows[:].unsqueeze(1).broadcast_to([P, QT, D]),
                                            ALU.add).then_inc(s_bo, 1)
                        if runs(i, 2):
                            normalize("pick", x3[q], 1.0, 1e-5, i, 2, q)
                        if runs(i, 1):
                            ch = Chain(pool, s_gchain, 4, i, 1, q)
                            plain(pool)
                            pool.wait_ge(s_gates, at(i, 1, q))
                            wait(pool, filled["gates_t"], at(i, 1, q, 1, -1))
                            gb = lambda k: gates_bf[:, :, k, :]
                            ch.link(g.tensor_copy(gb(0), gates[:]))
                            ch.join()
                            ch.link(g.tensor_tensor(gates_rest[:], gates[:], gb(0), ALU.subtract))
                            wait_apart(pool, s_gchain, ch.base + ch.n)
                            ch.link(g.tensor_copy(gb(1), gates_rest[:]))
                            ch.join()
                            ch.link(g.tensor_tensor(gb(2), gates_rest[:], gb(1), ALU.subtract))
                            ch.end()
                        if runs(i, 0):
                            pool.wait_ge(s_rden, at(i, 0, q))
                            pv = probs[:].rearrange("p m t n -> p m (t n)")
                            g.tensor_tensor(pv, pv, ssum[:].unsqueeze(2).broadcast_to([P, 32, 32]),
                                            ALU.mult).then_inc(s_probs, 1)
                        if runs(i, 1):
                            normalize("conv", x2[q], 1.0, 1e-6, i, 1, q)
                            wait(pool, drained["scan_out"], at(i, 2, q))
                            g.tensor_tensor(x2_bc[q][:], x2[q][:], bcon_rows[:].unsqueeze(1).broadcast_to([P, QT, D]),
                                            ALU.add).then_inc(s_x2bc, 1)
                        if runs(i, 0):
                            normalize("ffn", x1[q], 1.0, 1e-5, i, 0, q)

                columns(pool, step)

            @block.scalar
            def _(act):
                s = nc.scalar
                act.dma_start(wexp_raw[:], W_exp).then_inc(s_weights, 16)
                for k in range(2):
                    act.dma_start(wcon_raw[:, k, :], W_con).then_inc(s_weights, 16)
                act.wait_ge(s_weights, 16 * N_LOADS)
                s.mul(bg_col[:], bg_col[:], 0.5).then_inc(s_act_setup, 1)
                s.mul(w_o[:], w_o[:], 0.5).then_inc(s_act_setup, 1)
                s.mul(bgate_col[:], bgate_col[:], 0.1).then_inc(s_act_setup, 1)
                act.wait_ge(s_wT, 3)
                s.copy(w_expand[:], shared[0][0:D, 0:P]).then_inc(s_act_setup, 1)
                s.mul(w_con[:], shared[0][:, P:P + D], 0.5).then_inc(s_act_setup, 1)
                s.copy(w_pick[:], shared[0][0:D, 2 * P:2 * P + EP]).then_inc(s_act_setup, 1)
                act.wait_ge(s_act_setup, 6)
                act.wait_ge(s_dve_setup, 8)

                def step(i):
                    for q in range(2):
                        bk = lambda name: shared[bank_of(q, name)]
                        if runs(i, 1):
                            act.wait_ge(filled["ffn_t"], at(i, 1, q))
                            wait(act, drained["spread3"], at(i, 2, q))
                            s.copy(tT[q][:], bk("ffn_t")[:]).then_inc(drained["ffn_t"], 1)
                        if runs(i, 0):
                            act.wait_ge(filled["att_t"], at(i, 0, q))
                            wait(act, s_scores, at(i, 1, q))
                            s.activation(zT[q][:], bk("att_t")[0:D, :], ACT.Identity, bias=lnb_col[:],
                                         scale=lnw_col[:]).then_inc(drained["att_t"], 1)
                            act.wait_ge(filled["k"], at(i, 0, q))
                            for j in range(4):
                                ins = s.mul(kT[q][:, j, :], bk("k")[:], head_of[:, j:j + 1])
                            ins.then_inc(drained["k"], 1)
                            act.wait_ge(filled["q"], at(i, 0, q))
                            s.copy(qT[q][:], bk("q")[:]).then_inc(drained["q"], 1)
                            act.wait_ge(filled["gate"], at(i, 0, q))
                            wait(act, s_og, at(i, 1, q))
                            s.activation(gT[q][:], bk("gate")[:], ACT.Tanh, bias=bg_col[:],
                                         scale=0.5).then_inc(drained["gate"], 1)
                            act.wait_ge(filled["v"], at(i, 0, q))
                            wait(act, s_o, at(i, 1, q))
                            s.copy(v_sb[q][:].rearrange("p t c -> p (t c)"), bk("v")[:]).then_inc(drained["v"], 1)
                        if runs(i, 1):
                            act.wait_ge(s_diff, at(i, 1, q))
                            s.activation(g2e[:], m2[:], ACT.Exp).then_inc(s_ratio, 1)
                        if runs(i, 0):
                            act.wait_ge(s_sub, at(i, 0, q))
                            s.activation(probs[:], probs[:], ACT.Exp, scale=float(C) ** -0.5).then_inc(s_exp, 1)
                        if runs(i, 1):
                            act.wait_ge(filled["gates_t"], at(i, 1, q))
                            wait(act, filled["expert"], at(i, 1, q, 1, -1))
                            s.copy(gatesT[:], bk("gates_t")[:].bitcast(BF16)[0:32, 0:QTOK]).then_inc(drained["gates_t"], 1)
                        if runs(i, 2):
                            act.wait_ge(filled["pick_t"], at(i, 2, q))
                            wait(act, filled["pick"], at(i, 2, q, 1, -1))
                            s.copy(lT[:], bk("pick_t")[0:D, :]).then_inc(drained["pick_t"], 1)
                            act.wait_ge(filled["pick"], at(i, 2, q))
                            dst = picks[:].rearrange("p g (a b) -> p a g b", b=B)[:, q * 32:(q + 1) * 32, :, bass.ds(i - 2, 1)]
                            src = bk("pick")[:, 0:32 * NG].rearrange("p (a g) -> p a g", g=NG).unsqueeze(3)
                            s.activation(dst, src, ACT.Identity, bias=gb_col[:]).then_inc(drained["pick"], 1)
                        if runs(i, 0):
                            act.wait_ge(s_o, at(i, 0, q))
                            wait(act, s_o_sum, at(i, 0, q, 1, -1))
                            for h in range(2):
                                for k in range(4):
                                    src = o_bank[k][:, 0:QT * 64].rearrange("p (t h i) -> p t h i", h=2, i=32)[:, :, h, :]
                                    ins = s.mul(o_half[:, h, k], src, odd_even[:, h:h + 1])
                            ins.then_inc(s_o_read, 1)
                        if runs(i, 1):
                            act.wait_ge(filled["conv_t"], at(i, 1, q))
                            wait(act, filled["expand"], at(i, 1, q, 1, -1))
                            s.copy(cT[:], bk("conv_t")[0:D, :]).then_inc(drained["conv_t"], 1)
                            act.wait_ge(filled["expand"], at(i, 1, q))
                            wait(act, s_gated, at(i, 2, 1))
                            half = slice(q * 32, (q + 1) * 32)
                            s.activation(gpre[:, :, half].rearrange("p n a -> p a n"), bk("expand")[:, 0:256].rearrange("p (a n) -> p a n", n=8),
                                         ACT.Identity, bias=bgate_col[:], scale=0.1)
                            s.activation(prim[:, :, half].rearrange("p n a -> p a n"), bk("expand")[:, 256:512].rearrange("p (a n) -> p a n", n=8),
                                         ACT.Identity, bias=bprim_col[:]).then_inc(drained["expand"], 1)
                    if runs(i, 1):
                        act.wait_ge(s_ema, at(i, 1, 1, 1) if 0 else (i - 1) + 1)
                        s.activation(ema_t[:], ema[:], ACT.Tanh, scale=0.5).then_inc(s_emat, 1)

                columns(act, step)

            @block.tensor
            def _(pe):
                t_ = nc.tensor
                pe.wait_ge(s_weights, 16 * N_LOADS)
                pe.wait_ge(s_pool_setup, 2)
                t_.transpose(shared[0][0:D, 0:P], wexp_raw[:], ident[:]).then_inc(s_wT, 1)
                t_.transpose(shared[0][:, P:P + D], wcon_raw[:].rearrange("o k h -> o (k h)"),
                             ident[0:D, 0:D]).then_inc(s_wT, 1)
                t_.transpose(shared[0][0:D, 2 * P:2 * P + EP], gw_raw[:], ident[0:EP, 0:EP]).then_inc(s_wT, 1)
                pe.wait_ge(s_act_setup, 6)
                pe.wait_ge(s_pool_setup, N_POOL_SETUP)
                pe.wait_ge(s_dve_setup, 8)

                def step(i):
                    for q in range(2):
                        bk = lambda name: shared[bank_of(q, name)]
                        tile = lambda t: slice(t * P, (t + 1) * P)
                        if runs(i, 2):
                            bank_free(pe, i, q, "scan_out")
                            pe.wait_ge(s_gated, at(i, 2, 1))
                            for t in range(QT):
                                ins = t_.matmul(bk("scan_out")[:, t * D:(t + 1) * D],
                                                gated[q][:].rearrange("p a n -> p (a n)")[:, tile(t)], w_con[:])
                            ins.then_inc(filled["scan_out"], 1)
                        if runs(i, 1):
                            bank_free(pe, i, q, "ffn_t")
                            pe.wait_ge(s_norm["ffn"], at(i, 1, q))
                            for t in range(QT):
                                ins = t_.transpose(bk("ffn_t")[:, tile(t)],
                                                   norm_twice[q][:, t].rearrange("p k d -> p (k d)"), ident[:])
                            ins.then_inc(filled["ffn_t"], 1)
                            bank_free(pe, i, q, "route")
                            pe.wait_ge(drained["ffn_t"], at(i, 1, q))
                            for t in range(QT):
                                ins = t_.matmul(bk("route")[:, t * NE:(t + 1) * NE], tT[q][0:D, tile(t)], w_router[:])
                            ins.then_inc(filled["route"], 1)
                        if runs(i, 0):
                            bank_free(pe, i, q, "att_t")
                            wait_apart(pe, s_norm["att"], at(i, 0, q))
                            for t in range(QT):
                                ins = t_.transpose(bk("att_t")[0:D, tile(t)], norm["att"][q][:, t, :], ident[:])
                            ins.then_inc(filled["att_t"], 1)
                            pe.wait_ge(drained["att_t"], at(i, 0, q))
                            for name, w in (("k", 1), ("q", 0), ("gate", 2)):
                                bank_free(pe, i, q, name)
                                t_.matmul(bk(name)[:], w_qkgv[:, w, :], zT[q][:]).then_inc(filled[name], 1)
                            bank_free(pe, i, q, "v")
                            for t in range(QT):
                                ins = t_.matmul(bk("v")[:, tile(t)], zT[q][:, tile(t)], w_qkgv[:, 3, :])
                            ins.then_inc(filled["v"], 1)
                            plain(pe)
                            pe.wait_ge(drained["k"], at(i, 0, q))
                            pe.wait_ge(drained["q"], at(i, 0, q))
                            wait(pe, s_sub, at(i, 0, q, 1, -1))
                            for t in range(QT):
                                for g in range(4):
                                    tok = slice(t * P + g * 32, t * P + (g + 1) * 32)
                                    for r in range(2):
                                        ins = t_.matmul(s_bank[r][g * 32:(g + 1) * 32, tile(t)],
                                                        qT[q][r * 64:(r + 1) * 64, tok],
                                                        kT[q][r * 64:(r + 1) * 64, :, tok],
                                                        tile_position=(r * 64, g * 32))
                            ins.then_inc(s_scores, 1)
                        if runs(i, 1):
                            bank_free(pe, i, q, "gates_t")
                            pe.wait_ge(s_gchain, at(i, 1, q, 4))
                            for t in range(QT):
                                ins = t_.transpose(bk("gates_t")[:].bitcast(BF16)[0:32, tile(t)],
                                                   gates_bf[:, t].rearrange("p k e -> p (k e)"), ident_bf[:])
                            ins.then_inc(filled["gates_t"], 1)
                            pe.wait_ge(drained["gates_t"], at(i, 1, q))
                            for j in range(NE // 2):
                                bank_free(pe, i, q, f"spread{j}")
                                t_.matmul(bk(f"spread{j}")[:], spread_sel[:, j].rearrange("p e d -> p (e d)"),
                                          gatesT[:]).then_inc(filled[f"spread{j}"], 1)
                            bank_free(pe, i, q, "expert")
                            pe.wait_ge(drained["spread3"], at(i, 1, q))
                            for t in range(QT):
                                o = bk("expert")[:, t * D:(t + 1) * D]
                                for k in range(3):
                                    t_.matmul(o, gatesT[:, tile(t)], b_expert_bf[:, k, :], start=(k == 0), stop=False)
                                for j in range(NE // 2):
                                    ins = t_.matmul(o, xg[:, j, tile(t)], w_expert[:, j, :], start=False, stop=(j == 3))
                            ins.then_inc(filled["expert"], 1)
                        if runs(i, 2):
                            plain(pe)
                            bank_free(pe, i, q, "pick_t")
                            pe.wait_ge(s_norm["pick"], at(i, 2, q))
                            for t in range(QT):
                                ins = t_.transpose(bk("pick_t")[0:D, tile(t)], norm["pick"][q][:, t, :], ident[:])
                            ins.then_inc(filled["pick_t"], 1)
                            plain(pe)
                            bank_free(pe, i, q, "pick")
                            pe.wait_ge(drained["pick_t"], at(i, 2, q))
                            for j in range(4):
                                mv_ = lT[:].rearrange("d (a g j) -> d a g j", g=NG, j=4)[:, :, :, j]
                                ins = t_.matmul(bk("pick")[j * EP:(j + 1) * EP, 0:32 * NG], w_pick[:], mv_,
                                                tile_position=(0, j * EP))
                            ins.then_inc(filled["pick"], 1)
                        if runs(i, 0):
                            plain(pe)
                            pe.wait_ge(s_probsT, at(i, 0, q))
                            pe.wait_ge(drained["v"], at(i, 0, q))
                            wait(pe, s_o_read, at(i, 0, q, 1, -1))
                            pT = probsT[:].rearrange("p (r t h) i -> p r t h i", r=2, t=QT)
                            for t in range(QT):
                                for k in range(4):
                                    for g in range(4):
                                        ins = t_.matmul(o_bank[g][k * 32:(k + 1) * 32, t * 64:(t + 1) * 64],
                                                        v_sb[q][g * 32:(g + 1) * 32, t, k * 32:(k + 1) * 32],
                                                        pT[g * 32:(g + 1) * 32, k // 2, t, 2 * (k % 2):2 * (k % 2) + 2, :],
                                                        tile_position=(g * 32, k * 32))
                            ins.then_inc(s_o, 1)
                            bank_free(pe, i, q, "att_out")
                            pe.wait_ge(s_og, at(i, 0, q))
                            for t in range(QT):
                                ins = t_.matmul(bk("att_out")[:, t * D:(t + 1) * D], ogT[:, tile(t)], w_o[:])
                            ins.then_inc(filled["att_out"], 1)
                        if runs(i, 1):
                            plain(pe)
                            bank_free(pe, i, q, "conv_t")
                            pe.wait_ge(s_norm["conv"], at(i, 1, q))
                            for t in range(QT):
                                ins = t_.transpose(bk("conv_t")[0:D, tile(t)], norm["conv"][q][:, t, :], ident[:])
                            ins.then_inc(filled["conv_t"], 1)
                            plain(pe)
                            bank_free(pe, i, q, "expand")
                            pe.wait_ge(drained["conv_t"], at(i, 1, q))
                            cv = cT[:].rearrange("d (a h n) -> d a h n", h=2, n=8)
                            for part, w in ((0, D), (1, 0)):
                                for h in range(2):
                                    ins = t_.matmul(bk("expand")[h * D:(h + 1) * D, part * 256:(part + 1) * 256],
                                                    w_expand[:, w:w + D], cv[:, :, h, :], tile_position=(0, h * D))
                            ins.then_inc(filled["expand"], 1)

                columns(pe, step)

            @block.vector
            def _(dve):
                v = nc.vector
                dve.wait_ge(s_pool_setup, N_POOL_SETUP)
                dve.wait_ge(s_weights, 16 * N_LOADS)
                v.memset(gated[0][:], 0.0)
                v.memset(gated[1][:], 0.0).then_inc(s_dve_setup, 1)
                v.tensor_reduce(head_of[:], block_of[:].rearrange("p (x j) -> p j x", j=4), AX.X, ALU.add).then_inc(s_dve_setup, 1)
                v.tensor_reduce(odd_even[:], block_of[:].rearrange("p (x j) -> p j x", j=2), AX.X, ALU.add).then_inc(s_dve_setup, 1)
                v.tensor_reduce(spread_sel8[:], spread_sel3[:].rearrange("p k e -> p e k"), AX.X, ALU.add).then_inc(s_dve_setup, 1)
                v.tensor_copy(b_expert_bf[:, 0, :], b_expert[:]).then_inc(s_dve_setup, 1)
                dve.wait_ge(s_dve_setup, 5)
                v.tensor_scalar(other_big[:], odd_even[:], -BIG, BIG, ALU.mult, ALU.add)
                v.tensor_copy(spread_sel[:].rearrange("p j e d -> p (j e) d"),
                              spread_sel8[:].unsqueeze(2).broadcast_to([32, NE, D]))
                v.tensor_tensor(b_rest[:], b_expert[:], b_expert_bf[:, 0, :], ALU.subtract).then_inc(s_dve_setup, 1)
                dve.wait_ge(s_dve_setup, 6)
                v.tensor_copy(b_expert_bf[:, 1, :], b_rest[:]).then_inc(s_dve_setup, 1)
                dve.wait_ge(s_dve_setup, 7)
                v.tensor_tensor(b_expert_bf[:, 2, :], b_rest[:], b_expert_bf[:, 1, :], ALU.subtract).then_inc(s_dve_setup, 1)
                dve.wait_ge(s_dve_setup, 8)

                def stats(kind, src, i, behind, q):
                    for t in range(QT):
                        ins = v.bn_stats(bn[kind][q][:, t, :], src[:, t, :])
                    ins.then_inc(s_bn[kind], 1)
                    wait_apart(dve, s_bn[kind], at(i, behind, q))
                    for t in range(QT):
                        ins = v.bn_aggr(mv[kind][q][:, t, :], bn[kind][q][:, t, :])
                    ins.then_inc(s_agg[kind], 1)

                def tok(ap):
                    return ap[:, 0:QT * D].rearrange("p (t d) -> p t d", d=D)

                def step(i):
                    for q in range(2):
                        bk = lambda name: shared[bank_of(q, name)]
                        if runs(i, 0):
                            dve.wait_ge(s_x[q], i * 128 + 128)
                            wait(dve, s_norm["att"], at(i, 1, q))
                            stats("att", x_in[q], i, 0, q)
                        if runs(i, 2):
                            dve.wait_ge(filled["scan_out"], at(i, 2, q))
                            dve.wait_ge(s_x2bc, at(i, 2, q))
                            wait(dve, s_x3_store[q], (i - 3) * 128 + 128)
                            wait(dve, s_norm["pick"], at(i, 3, q))
                            v.tensor_tensor(x3[q][:], tok(bk("scan_out")), x2_bc[q][:], ALU.add).then_inc(drained["scan_out"], 1)
                            dve.wait_ge(drained["scan_out"], at(i, 2, q))
                            stats("pick", x3[q], i, 2, q)
                        if runs(i, 1):
                            ch = Chain(dve, s_top, 15, i, 1, q)
                            dve.wait_ge(filled["route"], at(i, 1, q))
                            v.tensor_tensor(lg[:], bk("route")[:, 0:QT * NE].rearrange("p (t e) -> p t e", e=NE),
                                            rb_rows[:].unsqueeze(1).broadcast_to([P, QT, NE]), ALU.add).then_inc(drained["route"], 1)
                            dve.wait_ge(drained["route"], at(i, 1, q))
                            wide = lambda a: a[:].unsqueeze(2).broadcast_to([P, QT, NE])

                            def best(scores, m, pick):
                                ch.link(v.tensor_reduce(m[:], scores[:], AX.X, ALU.max))
                                ch.join()
                                ch.link(v.tensor_tensor(eq[:], scores[:], wide(m), ALU.is_equal))
                                ch.join()
                                ch.link(v.tensor_tensor(eq[:], eq[:], first_wins[:].unsqueeze(1).broadcast_to([P, QT, NE]), ALU.mult))
                                ch.join()
                                ch.link(v.tensor_reduce(mw[:], eq[:], AX.X, ALU.max))
                                ch.join()
                                ch.link(v.tensor_tensor(pick[:], eq[:], wide(mw), ALU.is_equal))
                                ch.join()

                            best(lg, m1, pick1)
                            ch.link(v.scalar_tensor_tensor(lg2[:], pick1[:], -BIG, lg[:], ALU.mult, ALU.add))
                            ch.join()
                            best(lg2, m2, pick2)
                            v.tensor_tensor(m2[:], m2[:], m1[:], ALU.subtract).then_inc(s_diff, 1)
                            dve.wait_ge(s_ratio, at(i, 1, q))
                            ch.link(v.tensor_scalar(gden[:], g2e[:], 1.0, None, ALU.add))
                            ch.join()
                            ch.link(v.reciprocal(g1v[:], gden[:]))
                            ch.join()
                            ch.link(v.tensor_tensor(g2v[:], g2e[:], g1v[:], ALU.mult))
                            ch.join()
                            v.tensor_tensor(pick1[:], pick1[:], wide(g1v), ALU.mult)
                            ch.link(v.tensor_tensor(pick2[:], pick2[:], wide(g2v), ALU.mult))
                            ch.join()
                            ch.end()
                            wait(dve, s_gchain, at(i, 1, q, 4, -4))
                            v.tensor_tensor(gates[:], pick1[:], pick2[:], ALU.add).then_inc(s_gates, 1)
                        if runs(i, 0):
                            ch = Chain(dve, s_smax_chain, 4, i, 0, q)
                            dve.wait_ge(s_scores, at(i, 0, q))
                            for r in range(2):
                                ins = v.tensor_reduce(smax[:, r * 16:(r + 1) * 16, :].rearrange("p m t -> p (m t)"),
                                                      s_bank[r][:].rearrange("p (m n) -> p m n", n=16), AX.X, ALU.max)
                            ch.link(ins)
                            ch.join()
                            ch.link(v.tensor_tensor(smax[:], smax[:], odd_even[:].unsqueeze(1).broadcast_to([P, 32, 2]), ALU.mult))
                            ch.join()
                            ch.link(v.tensor_tensor(smax[:], smax[:], other_big[:].unsqueeze(1).broadcast_to([P, 32, 2]), ALU.add))
                            ch.join()
                            wait(dve, s_probsT, at(i, 0, q, 1, -1))
                            for r in range(2):
                                ins = v.tensor_tensor(probs[:, r * 16:(r + 1) * 16].rearrange("p m t n -> p (m t) n"),
                                                      s_bank[r][:].rearrange("p (m n) -> p m n", n=16),
                                                      smax[:, r * 16:(r + 1) * 16, :].rearrange("p m t -> p (m t)").unsqueeze(2).broadcast_to([P, 32, 16]),
                                                      ALU.subtract)
                            ins.then_inc(s_sub, 1)
                            dve.wait_ge(s_exp, at(i, 0, q))
                            ch.link(v.tensor_reduce(ssum[:], probs[:].rearrange("p m t n -> p m (t n)"), AX.X, ALU.add))
                            ch.join()
                            ch.end()
                            v.reciprocal(ssum[:], ssum[:]).then_inc(s_rden, 1)
                        if runs(i, 1):
                            for j in range(NE // 2):
                                dve.wait_ge(filled[f"spread{j}"], at(i, 1, q))
                                if j == 0:
                                    wait(dve, filled["expert"], at(i, 1, q, 1, -1))
                                v.tensor_tensor(xg[:, j, :], bk(f"spread{j}")[:], tT[q][:], ALU.mult).then_inc(drained[f"spread{j}"], 1)
                        if runs(i, 0):
                            dve.wait_ge(s_probs, at(i, 0, q))
                            wait(dve, s_o, at(i, 0, q, 1, -1))
                            v.transpose(probsT[:].rearrange("p m i -> p (m i)"),
                                        probs[:].rearrange("p m t n -> p (m t n)")).then_inc(s_probsT, 1)
                        if runs(i, 1):
                            dve.wait_ge(filled["expert"], at(i, 1, q))
                            wait(dve, s_x2bc, at(i, 2, q))
                            v.tensor_tensor(x2[q][:], tok(bk("expert")), x1[q][:], ALU.add).then_inc(drained["expert"], 1)
                            dve.wait_ge(drained["expert"], at(i, 1, q))
                            stats("conv", x2[q], i, 1, q)
                        if runs(i, 0):
                            dve.wait_ge(s_o_read, at(i, 0, q))
                            oT4 = oT[:].rearrange("p (t g i) -> p g t i", g=4, i=32)
                            v.tensor_tensor(oT4, o_half[:, 0], o_half[:, 1], ALU.add).then_inc(s_o_sum, 1)
                            dve.wait_ge(s_o_sum, at(i, 0, q))
                            dve.wait_ge(drained["gate"], at(i, 0, q))
                            wait(dve, filled["att_out"], at(i, 0, q, 1, -1))
                            v.scalar_tensor_tensor(ogT[:], gT[q][:], 1.0, oT[:], ALU.add, ALU.mult).then_inc(s_og, 1)
                            dve.wait_ge(filled["att_out"], at(i, 0, q))
                            dve.wait_ge(s_bo, at(i, 0, q))
                            wait(dve, s_norm["ffn"], at(i, 1, q))
                            v.tensor_tensor(x1[q][:], tok(bk("att_out")), x_bo[q][:], ALU.add).then_inc(drained["att_out"], 1)
                            dve.wait_ge(drained["att_out"], at(i, 0, q))
                            stats("ffn", x1[q], i, 0, q)
                    if runs(i, 1):
                        dve.wait_ge(drained["expand"], at(i, 1, 1))
                        wait(dve, s_emat, i - 1)
                        v.tensor_tensor_scan(ema[:].rearrange("p n a -> p (n a)"), decay[:].rearrange("p n a -> p (n a)"),
                                             gpre[:].rearrange("p n a -> p (n a)"), 0.0, ALU.mult, ALU.add).then_inc(s_ema, 1)
                        dve.wait_ge(s_emat, (i - 1) + 1)
                        wait(dve, filled["scan_out"], at(i, 2, 1))
                        for q in range(2):
                            for h in range(2):
                                rows = slice(h * D, (h + 1) * D)
                                half = slice(q * 32, (q + 1) * 32)
                                ins = v.scalar_tensor_tensor(gated[q][rows, :, h * 8:(h + 1) * 8], ema_t[rows, :, half].rearrange("p n a -> p a n"), 1.0,
                                                             prim[rows, :, half].rearrange("p n a -> p a n"), ALU.add, ALU.mult)
                            ins.then_inc(s_gated, 1)

                columns(dve, step)

        with ExitStack() as imgs:
            def ib(name, shape, dt=F32):
                return sb(name, shape, dt, imgs)

            w1 = ib("w1", [D + 1, EP, HID])
            w2 = ib("w2", [P, 2, EP, D])
            w2b = ib("w2b", [1, EP, D])
            ones_row = ib("ones_row", [1, N])
            best8, best8e = ib("best8", [P, 8]), ib("best8e", [P, 8])
            neg_max, psum_, prec = ib("neg_max", [P, 1]), ib("psum_", [P, 1]), ib("prec", [P, 1])
            rest = ib("rest", [P, TOK])
            wT = ib("wT", [P, IT, P])
            xi = pair("xi", [P, IT, D], F32, imgs)
            ibn, imv, irstd = ib("ibn", [P, IT, 6]), ib("imv", [P, IT, 2]), ib("irstd", [P, 2, IT])
            iminus = ib("iminus", [P, IT])
            pooled = ib("pooled", [D + 1, N, EP])
            hidT = ib("hidT", [P, EP, 2, N])
            eoT = ib("eoT", [D, N, EP])
            eo = ib("eo", [P, NG, D])
            s_w = sem("w4_loaded")
            s_c = sem("c4_ready")
            s_max, s_neg, s_e, s_eb, s_rec, s_scaled, s_rep, s_wts = (sem("g_max"), sem("g_neg"), sem("g_exp"), sem("g_exp8"), sem("g_rec"),
                                                                     sem("g_scaled"), sem("g_replaced"), sem("g_weights"))
            s_wt_ps, s_wt_cp = sem("wT_filled"), sem("wT_copied")
            s_xi = [sem(f"xi_loaded{b}") for b in range(2)]
            s_xo = [sem(f"xo_stored{b}") for b in range(2)]
            s_ibn, s_iagg, s_ipn, s_inorm, s_pool_mm, s_pool_cp = (sem("i_stats"), sem("i_agg"), sem("i_pn"), sem("i_norm"),
                                                                   sem("i_pooled"), sem("i_pooled_copied"))
            s_hid, s_gelu, s_eo1, s_eo1c, s_eo2, s_eo2c = (sem("hid_filled"), sem("gelu_done"), sem("eoT_filled"), sem("eoT_copied"),
                                                            sem("eo_filled"), sem("eo_copied"))
            s_add_ps, s_added = sem("add_filled"), sem("added")

            block = imgs.enter_context(nc.Block())

            @block.sync
            def _(sp):
                sp.dma_start(w1[:], weight1.rearrange("e d h -> d e h")).then_inc(s_w, 16)
                for c in range(2):
                    sp.dma_start(w2[:, c], weight2[:, c * P:(c + 1) * P, :].rearrange("e h o -> h e o")).then_inc(s_w, 16)
                sp.dma_start(w2b[:], weight2[:, HID:HID + 1, :].rearrange("e one o -> one e o")).then_inc(s_w, 16)
                for n in range(N):
                    if n >= 2:
                        sp.wait_ge(s_pool_mm, n - 1)
                    sp.dma_start(xi[n % 2][:].rearrange("p t d -> p (t d)"), x3_imgs[n]).then_inc(s_xi[n % 2], 16)
                for n in range(N):
                    if n < 2:
                        sp.wait_ge(s_pool_mm, N - 1 + n)
                    else:
                        sp.wait_ge(s_xo[n % 2], 16 * (n // 2))
                    sp.dma_start(xi[n % 2][:].rearrange("p t d -> p (t d)"), x3_imgs[n]).then_inc(s_xi[n % 2], 16)
                    if n >= 1:
                        sp.wait_ge(s_added, 4 * n)
                        sp.dma_start(out_imgs[n - 1], xi[(n - 1) % 2][:].rearrange("p t d -> p (t d)")).then_inc(s_xo[(n - 1) % 2], 16)
                sp.wait_ge(s_added, 4 * N)
                sp.dma_start(out_imgs[N - 1], xi[(N - 1) % 2][:].rearrange("p t d -> p (t d)")).then_inc(s_xo[(N - 1) % 2], 16)
                for b in range(2):
                    sp.wait_ge(s_xo[b], 16 * N // 2)

            @block.gpsimd
            def _(pool):
                g = nc.gpsimd
                g.memset(iminus[:], -0.5).then_inc(s_c, 1)
                g.memset(ones_row[:], 1.0).then_inc(s_c, 1)
                pool.wait_ge(s_c, 2)
                g.memset(pooled[D:D + 1], 1.0).then_inc(s_c, 1)
                pool.wait_ge(s_c, 3)
                for n in range(N):
                    pool.wait_ge(s_iagg, n + 1)
                    g.tensor_tensor(xi[n % 2][:], xi[n % 2][:], imv[:, :, 0:1].broadcast_to([P, IT, D]), ALU.subtract)
                    g.tensor_scalar(irstd[:, 0, :], imv[:, :, 1], 1.0, 1e-5, ALU.mult, ALU.add).then_inc(s_ipn, 1)
                    pool.wait_ge(s_ipn, 2 * n + 1)
                    g.tensor_tensor(irstd[:, 1, :], irstd[:, 0, :], iminus[:], ALU.pow).then_inc(s_ipn, 1)
                    pool.wait_ge(s_ipn, 2 * n + 2)
                    g.tensor_tensor(xi[n % 2][:], xi[n % 2][:], irstd[:, 1, :].unsqueeze(2).broadcast_to([P, IT, D]),
                                    ALU.mult).then_inc(s_inorm, 1)

            @block.scalar
            def _(act):
                s = nc.scalar
                for gr in range(NG):
                    act.wait_ge(s_neg, gr + 1)
                    s.activation(picks[:, gr, :], picks[:, gr, :], ACT.Exp, bias=neg_max[:], accum_out=psum_[:]).then_inc(s_e, 1)
                    if gr:
                        act.wait_ge(s_wts, gr)
                    s.activation(best8e[:], best8[:], ACT.Exp, bias=neg_max[:]).then_inc(s_e, 1)
                    act.wait_ge(s_rec, gr + 1)
                    s.mul(picks[:, gr, :], picks[:, gr, :], prec[:])
                    s.mul(best8e[:], best8e[:], prec[:]).then_inc(s_scaled, 1)
                    for u in range(IT // 4):
                        act.wait_ge(s_wt_ps, gr * (IT // 4) + u + 1)
                        if u == 0 and gr:
                            act.wait_ge(s_pool_mm, 4 * gr)
                        s.copy(wT[:, 4 * u:4 * u + 4, :].rearrange("p t m -> p (t m)"), banks[u % 2][:]).then_inc(s_wt_cp, 1)
                act.wait_ge(s_pool_mm, N)
                s.copy(pooled[0:D].rearrange("p n e -> p (n e)"), banks[2][0:D, :]).then_inc(s_pool_cp, 1)
                for u in range(2):
                    act.wait_ge(s_hid, u + 1)
                    s.activation(hidT[:, 16 * u:16 * u + 16].rearrange("p e c n -> p (e c n)"), banks[3 + u][:], ACT.Gelu).then_inc(s_gelu, 1)
                act.wait_ge(s_eo1, 1)
                s.copy(eoT[:].rearrange("p n e -> p e n"), banks[5][0:D, :].rearrange("p (e n) -> p e n", n=N)).then_inc(s_eo1c, 1)
                act.wait_ge(s_eo2, 1)
                s.copy(eo[:].rearrange("p g d -> p (g d)"), banks[6][:, 0:NG * D]).then_inc(s_eo2c, 1)

            @block.tensor
            def _(pe):
                t_ = nc.tensor
                pe.wait_ge(s_c, 3)
                for gr in range(NG):
                    pe.wait_ge(s_wts, gr + 1)
                    wv = picks[:, gr, :].rearrange("p (m t) -> p t m", t=IT)
                    for u in range(IT // 4):
                        if gr * (IT // 4) + u >= 2:
                            pe.wait_ge(s_wt_cp, gr * (IT // 4) + u - 1)
                        for t in range(4):
                            ins = t_.transpose(banks[u % 2][:, t * P:(t + 1) * P], wv[:, 4 * u + t, :], ident[:])
                        ins.then_inc(s_wt_ps, 1)
                    pe.wait_ge(s_wt_cp, (gr + 1) * (IT // 4))
                    for j in range(4):
                        n = 4 * gr + j
                        pe.wait_ge(s_inorm, n + 1)
                        for t in range(IT):
                            ins = t_.matmul(banks[2][0:D, n * EP:(n + 1) * EP], xi[n % 2][:, t, :], wT[:, t, j * EP:(j + 1) * EP],
                                            start=(t == 0), stop=(t == IT - 1))
                        ins.then_inc(s_pool_mm, 1)
                pe.wait_ge(s_w, 64)
                pe.wait_ge(s_pool_cp, 1)
                for e in range(EP):
                    for c in range(2):
                        ins = t_.matmul(banks[3 + e // 16][:, ((e % 16) * 2 + c) * N:((e % 16) * 2 + c + 1) * N],
                                        w1[:, e, c * P:(c + 1) * P], pooled[:, :, e])
                    if e % 16 == 15:
                        ins.then_inc(s_hid, 1)
                for e in range(EP):
                    if e % 16 == 0:
                        pe.wait_ge(s_gelu, e // 16 + 1)
                    o = banks[5][0:D, e * N:(e + 1) * N]
                    for c in range(2):
                        t_.matmul(o, w2[:, c, e, :], hidT[:, e, c, :], start=(c == 0), stop=False)
                    ins = t_.matmul(o, w2b[:, e, :], ones_row[:], start=False, stop=True)
                ins.then_inc(s_eo1, 1)
                pe.wait_ge(s_eo1c, 1)
                for gr in range(NG):
                    ins = t_.transpose(banks[6][:, gr * D:(gr + 1) * D], eoT[:, 4 * gr:4 * gr + 4, :].rearrange("p n e -> p (n e)"),
                                       ident[0:D, 0:D])
                ins.then_inc(s_eo2, 1)
                pe.wait_ge(s_eo2c, 1)
                for n in range(N):
                    gr, j = n // 4, n % 4
                    wv = picks[:, gr, :].rearrange("p (m t) -> p t m", t=IT)
                    for u in range(4):
                        if 4 * n + u >= 8:
                            pe.wait_ge(s_added, 4 * n + u - 7)
                        for t in range(8):
                            ins = t_.matmul(banks[(4 * n + u) % 8][:, t * D:(t + 1) * D], wv[j * EP:(j + 1) * EP, 8 * u + t, :],
                                            eo[j * EP:(j + 1) * EP, gr, :], tile_position=(j * EP, 0))
                        ins.then_inc(s_add_ps, 1)

            @block.vector
            def _(dve):
                v = nc.vector
                dve.wait_ge(s_c, 3)

                def image_stats(n):
                    dve.wait_ge(s_xi[n % 2], 16 * (n // 2 + 1))
                    if n:
                        dve.wait_ge(s_inorm, n)
                    for t in range(IT):
                        ins = v.bn_stats(ibn[:, t, :], xi[n % 2][:, t, :])
                    ins.then_inc(s_ibn, 1)
                    dve.wait_ge(s_ibn, n + 1)
                    for t in range(IT):
                        ins = v.bn_aggr(imv[:, t, :], ibn[:, t, :])
                    ins.then_inc(s_iagg, 1)

                for gr in range(NG):
                    v.max(best8[:], picks[:, gr, :]).then_inc(s_max, 1)
                    dve.wait_ge(s_max, gr + 1)
                    v.tensor_scalar(neg_max[:], best8[:, 0:1], -1.0, None, ALU.mult).then_inc(s_neg, 1)
                    image_stats(4 * gr)
                    dve.wait_ge(s_e, 2 * gr + 2)
                    v.reciprocal(prec[:], psum_[:]).then_inc(s_rec, 1)
                    image_stats(4 * gr + 1)
                    dve.wait_ge(s_scaled, gr + 1)
                    v.match_replace(rest[:], best8e[:], picks[:, gr, :], 0.0).then_inc(s_rep, 1)
                    dve.wait_ge(s_rep, gr + 1)
                    v.tensor_tensor(picks[:, gr, :], picks[:, gr, :], rest[:], ALU.subtract).then_inc(s_wts, 1)
                    dve.wait_ge(s_wts, gr + 1)
                    image_stats(4 * gr + 2)
                    image_stats(4 * gr + 3)
                for n in range(N):
                    dve.wait_ge(s_xi[n % 2], 16 * (N // 2 + n // 2 + 1))
                    for u in range(4):
                        dve.wait_ge(s_add_ps, 4 * n + u + 1)
                        xs = xi[n % 2][:, 8 * u:8 * u + 8, :].rearrange("p t d -> p (t d)")
                        v.tensor_tensor(xs, xs, banks[(4 * n + u) % 8][:], ALU.add).then_inc(s_added, 1)


_INS = ['x', 'L0_conv_ln_w', 'L0_conv_ln_b', 'L0_conv_Wq', 'L0_conv_Wk', 'L0_conv_Wv', 'L0_conv_Wg', 'L0_conv_bg',
        'L0_conv_Wo', 'L0_conv_bo', 'L0_ffn_router_w', 'L0_ffn_router_b', 'L0_ffn_expert_w', 'L0_ffn_expert_b',
        'L1_conv_W_exp', 'L1_conv_b_exp', 'L1_conv_W_con', 'L1_conv_b_con', 'L1_ffn_gate_w', 'L1_ffn_gate_b',
        'L1_ffn_weight1', 'L1_ffn_weight2']


def kernel(**inputs):
    import numpy as np
    import concourse.bacc as bacc
    from concourse import mybir as mb
    from concourse.bass_utils import run_bass_kernel_spmd

    nc = bacc.Bacc("TRN2", target_bir_lowering=False, num_devices=1)
    arrays, args = {}, []
    for name in _INS:
        a = np.ascontiguousarray(inputs[name])
        arrays[f"in_{name}"] = a
        args.append(nc.dram_tensor(f"in_{name}", a.shape, mb.dt.from_np(a.dtype), kind="ExternalInput").ap())
    out = nc.dram_tensor("out_x", inputs["x"].shape, mb.dt.float32, kind="ExternalOutput").ap()
    build(nc, *args, out)
    r = run_bass_kernel_spmd(nc, [arrays], core_ids=[0])
    return r.results[0]["out_x"]
```

```python
from contextlib import ExitStack

import concourse.bass as bass
from concourse import mybir

ALU = mybir.AluOpType
ACT = mybir.ActivationFunctionType
AX = mybir.AxisListType
F32 = mybir.dt.float32
F32R = mybir.dt.float32r
BF16 = mybir.dt.bfloat16

P = 128
QT = 4
QTOK = QT * P
BIG = 1e30

LAG = {"att_norm": 0, "att_t": 1, "k": 1, "q": 1, "gate": 1, "v": 1, "scores": 1,
       "values": 2, "att_out": 2, "ffn_t": 3, "route": 3, "y0": 3, "y1": 3, "y2": 3, "y3": 3,
       "mix": 4, "conv_t": 4, "expand": 4, "scan_out": 6, "pick_t": 6, "pick": 6, "n3_store": 7}
TURNS = ["att_t", "scan_out", "k", "q", "gate", "v", "ffn_t", "conv_t", "route", "expand",
         "y0", "y1", "att_out", "y2", "y3", "pick_t", "pick"]
PEELED = 4


def build(nc, x, ln_w, ln_b, Wq, Wk, Wv, Wg, bg, Wo, bo, router_w, router_b, expert_w, expert_b,
          W_exp, b_exp, W_con, b_con, gate_w, gate_b, weight1, weight2, out):
    N, A, B, D = x.shape
    HC = Wq.shape[1]
    H = 8
    C = HC // H
    NE = router_w.shape[1]
    EP, HID = gate_w.shape[0], weight1.shape[2]
    TOK = A * B
    NG = N // 4
    IT = TOK // P
    HALVES = 2 * B
    assert HC == P and N == 16 and D == 64 and A == 64 and B == 64 and EP == 32

    def cols_of(ap):
        return ap.rearrange("n (q t p) b d -> p q b n t d", q=2, t=QT)

    def imgs_of(ap):
        return ap.rearrange("n a b d -> n (a b d)").rearrange("n (p f) -> n p f", p=P)

    x3_dram = nc.dram_tensor("x3_scratch", [N, A, B, D], F32).ap()
    n3_dram = nc.dram_tensor("normalized_x3_scratch", [N, A, B, D], F32).ap()
    x_cols, x3_cols, n3_cols = cols_of(x), cols_of(x3_dram), cols_of(n3_dram)
    x3_imgs, n3_imgs, out_imgs = imgs_of(x3_dram), imgs_of(n3_dram), imgs_of(out)

    with ExitStack() as ctx:
        def sb(name, shape, dt=F32, c=ctx):
            return c.enter_context(nc.sbuf_tensor(name, shape, dt))

        def pair(name, shape, dt=F32, c=ctx):
            return [sb(f"{name}{q}", shape, dt, c) for q in range(2)]

        def sem(name):
            return ctx.enter_context(nc.semaphore(name))

        ident = sb("ident", [P, P])
        picks = sb("picks", [P, NG, TOK])
        shared = [ctx.enter_context(nc.psum_tensor(f"shared{i}", [P, 512], F32)) for i in range(2)]
        s_bank = ctx.enter_context(nc.psum_tensor("s_bank", [P, 2, 512], F32))
        o_bank = ctx.enter_context(nc.psum_tensor("o_bank", [P, 4, 512], F32))

        with ExitStack() as cols:
            def cb(name, shape, dt=F32):
                return sb(name, shape, dt, cols)

            def cpair(name, shape, dt=F32):
                return pair(name, shape, dt, cols)

            lnw_col, lnb_col, bg_col = cb("lnw_col", [P, 1]), cb("lnb_col", [P, 1]), cb("bg_col", [P, 1])
            w_raw = cb("w_raw", [P, 4, HC])
            w_qkg_hi, w_qkg_lo = cb("w_qkg_hi", [P, 3, HC], F32R), cb("w_qkg_lo", [P, 3, HC], F32R)
            w_scaled = cb("w_scaled", [P, 4, HC])
            b_qkg = cb("b_qkg", [P, 3])
            b_k = cb("b_k", [P, 4])
            w_o = cb("w_o", [P, D])
            w_o2 = cb("w_o2", [P, 2, D])
            bo_rows, bcon_rows, rb_rows = cb("bo_rows", [P, D]), cb("bcon_rows", [P, D]), cb("rb_rows", [P, NE])
            w_router = cb("w_router", [P, NE])
            w_expert = cb("w_expert", [P, NE, D])
            w_expert_hi, w_expert_lo = cb("w_expert_hi", [P, NE * D], F32R), cb("w_expert_lo", [P, NE * D], F32R)
            bias_row = cb("bias_row", [1, NE * D + HC])
            bias_rest = cb("bias_rest", [1, NE * D + HC])
            bias_parts = cb("bias_parts", [1, 3, NE * D + HC], BF16)
            bias3 = cb("bias3", [3, NE * D + HC], BF16)
            ones3 = cb("ones3", [3, P], BF16)
            wexp_raw, wcon_raw, gw_raw = cb("wexp_raw", [2 * D, 2, D]), cb("wcon_raw", [D, 2, D]), cb("gw_raw", [EP, D])
            w_expand_hi, w_expand_lo = cb("w_expand_hi", [P, 2 * D], F32R), cb("w_expand_lo", [P, 2 * D], F32R)
            w_con = cb("w_con", [P, D])
            w_pick = cb("w_pick", [D, EP])
            bprim_col, bgate_col, gb_col = cb("bprim_col", [P, 1]), cb("bgate_col", [P, 1]), cb("gb_col", [P, 1])
            block_of = cb("block_of", [P, 8])
            head_of = cb("head_of", [P, 4])
            odd_even = cb("odd_even", [P, 2])
            other_big = cb("other_big", [P, 2])
            decay = cb("decay", [P, 8, A])
            first_wins = cb("first_wins", [P, NE])
            minus_half = cb("minus_half", [P, QT])

            x_in = cpair("x_in", [P, QT, D])
            x_bo = cpair("x_bo", [P, QT, D])
            x1 = cpair("x1", [P, QT, D])
            x2 = cpair("x2", [P, QT, D])
            x2_bc = cpair("x2_bc", [P, QT, D])
            x3 = cpair("x3", [P, QT, D])
            KINDS = ("att", "ffn", "conv", "pick")
            norm = {k: cpair(f"norm_{k}", [P, QT, D]) for k in KINDS}
            split = {k: cpair(f"split_{k}", [P, QT, 2, D], F32R) for k in KINDS[:3]}
            bn = {k: cpair(f"bn_{k}", [P, QT, 6]) for k in KINDS}
            mv = {k: cpair(f"mv_{k}", [P, QT, 2]) for k in KINDS}
            rstd = {k: cpair(f"rstd_{k}", [P, 2, QT]) for k in KINDS}
            zT = cpair("zT", [P, QTOK], F32R)
            qT = cpair("qT", [P, QTOK])
            kT = cpair("kT", [P, 4, QTOK])
            gT = cpair("gT", [P, QTOK])
            v_sb = cpair("v_sb", [P, QT, HC])
            probs = cb("probs", [P, 32, 2, 16])
            probsT = cb("probsT", [P, 32, 32])
            smax = cb("smax", [P, 32, 2])
            ssum = cb("ssum", [P, 32])
            ogT = cb("ogT", [P, 2, QTOK])
            tT = cpair("tT", [P, QTOK], F32R)
            lg = cb("lg", [P, QT, NE])
            pick1, pick2 = cb("pick1", [P, QT, NE]), cb("pick2", [P, QT, NE])
            lg2, eq = cb("lg2", [P, QT, NE]), cb("eq", [P, QT, NE])
            m1, m2, mw = cb("m1", [P, QT]), cb("m2", [P, QT]), cb("mw", [P, QT])
            g2e, g1v, g2v, gden = cb("g2e", [P, QT]), cb("g1v", [P, QT]), cb("g2v", [P, QT]), cb("gden", [P, QT])
            gates = cb("gates", [P, QT, NE])
            yg = cb("yg", [P, QT, NE, D])
            mixed = cb("mixed", [P, QT, D])
            cT = cb("cT", [P, QTOK], F32R)
            prim, gpre = cb("prim", [P, 8, A]), cb("gpre", [P, 8, A])
            ema, ema_t = cb("ema", [P, 8, A]), cb("ema_t", [P, 8, A])
            gated = cpair("gated", [P, A // 2, N])
            lT = cb("lT", [D, QTOK])

            s_weights, s_pool_setup, s_dve_setup = sem("weights_loaded"), sem("pool_setup"), sem("dve_setup")
            s_pe_setup, s_act_setup, s_bias3 = sem("pe_setup"), sem("act_setup"), sem("bias3_loaded")
            filled = {k: sem(f"filled_{k}") for k in TURNS}
            drained = {k: sem(f"drained_{k}") for k in TURNS}
            s_x = [sem(f"x_loaded{q}") for q in range(2)]
            s_bo = sem("x_bo_done")
            s_bn = {k: sem(f"stats_{k}") for k in KINDS}
            s_agg = {k: sem(f"aggregated_{k}") for k in KINDS}
            s_pn = {k: sem(f"pool_norm_{k}") for k in KINDS}
            s_norm = {k: sem(f"normalized_{k}") for k in KINDS}
            s_hi = {k: sem(f"rounded_{k}") for k in KINDS[:3]}
            s_split = {k: sem(f"split_{k}") for k in KINDS[:3]}
            s_scores, s_sub, s_exp, s_rden, s_probs, s_probsT = (sem("scores_filled"), sem("scores_read"), sem("exp_done"),
                                                                 sem("denominators"), sem("probs_normalized"), sem("probs_transposed"))
            s_smax_chain, s_o, s_og, s_gp1 = sem("softmax_chain"), sem("o_filled"), sem("o_gated"), sem("gate_plus_one")
            s_top, s_diff, s_ratio, s_gates = sem("top_chain"), sem("top_diff"), sem("top_ratio"), sem("gates_done")
            s_sums = sem("exp_summed")
            s_mixed, s_x2, s_x2bc = sem("experts_mixed"), sem("x2_done"), sem("x2_bc_done")
            s_ema, s_emat, s_gated = sem("ema_done"), sem("ema_tanh"), sem("gated_done")
            s_x3_store = [sem(f"x3_stored{q}") for q in range(2)]
            s_n3_store = [sem(f"n3_stored{q}") for q in range(2)]

            N_LOADS = 34
            N_POOL_SETUP = 17
            N_DVE_SETUP = 13

            def at(i, q, lag, n=1, more=0):
                return i * (2 * n) + ((q - lag + 1) * n + more)

            def par(q, lag):
                return (q - lag) % 2

            def column(i, q, lag):
                return i + (q - lag - par(q, lag)) // 2

            def wait(eng, s, value):
                if not isinstance(value, int) or value > 0:
                    eng.wait_ge(s, value)

            def plain(eng):
                eng.wait_ge(s_pool_setup, N_POOL_SETUP)

            def wait_apart(eng, *waits):
                held = [(sem_, value if isinstance(value, int) else eng.to_reg(value)) for sem_, value in waits]
                plain(eng)
                for sem_, value in held:
                    wait(eng, sem_, value)

            def runs(i, q, lag):
                return not isinstance(i, int) or 0 <= 2 * i + q - lag < HALVES

            def bank_of(q, name):
                return (len(TURNS) * q + TURNS.index(name)) % 2

            def last_drained(i, q, name):
                pos = len(TURNS) * q + TURNS.index(name)
                for back in range(pos - 2, pos - 6 * len(TURNS), -2):
                    slots_back, turn = divmod(back, len(TURNS))
                    prev = TURNS[turn]
                    if not isinstance(i, int) or 0 <= 2 * i + slots_back - LAG[prev] < HALVES:
                        return drained[prev], at(i, slots_back, LAG[prev])
                return drained["pick"], 0

            def bank_free(pe, i, q, name):
                wait(pe, *last_drained(i, q, name))

            class Chain:

                def __init__(self, eng, s, per, i, q, lag):
                    self.eng, self.s, self.per, self.n = eng, s, per, 0
                    self.base = at(i, q, lag, per) - per

                def link(self, ins):
                    self.n += 1
                    ins.then_inc(self.s, 1)

                def join(self):
                    self.eng.wait_ge(self.s, self.base + self.n)

                def end(self):
                    assert self.n == self.per, (self.n, self.per)

            def n3_stored(i, q, lag):
                return (column(i, q, lag) + 1) * 128

            def slots(engine, step):
                for i in range(PEELED):
                    for q in range(2):
                        step(i, q)
                with engine.Fori(PEELED, B) as i:
                    for q in range(2):
                        step(i, q)
                for i in range(B, B + (max(LAG.values()) + 1) // 2):
                    for q in range(2):
                        step(i, q)

            block = cols.enter_context(nc.Block())

            @block.sync
            def _(sp):
                loads = [(bg_col[:], bg.unsqueeze(1)), (w_o[:], Wo),
                         (bo_rows[:], bo.unsqueeze(0).broadcast_to([P, D])),
                         (bcon_rows[:], b_con.unsqueeze(0).broadcast_to([P, D])),
                         (rb_rows[:], router_b.unsqueeze(0).broadcast_to([P, NE])),
                         (gw_raw[:], gate_w),
                         (bias_row[:, 0:NE * D], expert_b.rearrange("e c -> (e c)").unsqueeze(0))]
                be = b_exp.rearrange("(h d) -> h d", h=2).unsqueeze(2)
                for k in range(2):
                    rows = slice(k * D, (k + 1) * D)
                    loads += [(lnw_col[rows], ln_w.unsqueeze(1)), (lnb_col[rows], ln_b.unsqueeze(1)),
                              (w_raw[rows, 0, :], Wq), (w_raw[rows, 1, :], Wk), (w_raw[rows, 2, :], Wg), (w_raw[rows, 3, :], Wv),
                              (w_router[rows], router_w), (w_expert[rows], expert_w.rearrange("e d c -> d e c")),
                              (bprim_col[rows], be[0]), (bgate_col[rows], be[1])]
                loads += [(gb_col[k * EP:(k + 1) * EP], gate_b.unsqueeze(1)) for k in range(4)]
                for dst, src in loads:
                    sp.dma_start(dst, src).then_inc(s_weights, 16)
                assert len(loads) + 3 == N_LOADS, len(loads)
                sp.wait_ge(s_dve_setup, N_DVE_SETUP)
                sp.dma_start(bias3[:], bias_parts[:]).then_inc(s_bias3, 16)

                def step(i, q):
                    if runs(i, q, 0):
                        wait(sp, s_bo, at(i, q, 2))
                        for p in range(8):
                            sp.dma_start(x_in[q][p * N:(p + 1) * N], x_cols[p, q, i]).then_inc(s_x[q], 16)
                    lag = LAG["n3_store"]
                    if runs(i, q, lag):
                        z = par(q, lag)
                        sp.wait_ge(s_norm["pick"], at(i, q, lag))
                        for p in range(8):
                            sp.dma_start(n3_cols[p, z, column(i, q, lag)],
                                         norm["pick"][z][p * N:(p + 1) * N]).then_inc(s_n3_store[z], 16)
                    lag = LAG["scan_out"]
                    if runs(i, q, lag):
                        z = par(q, lag)
                        sp.wait_ge(drained["scan_out"], at(i, q, lag))
                        for p in range(8):
                            sp.dma_start(x3_cols[p, z, column(i, q, lag)], x3[z][p * N:(p + 1) * N]).then_inc(s_x3_store[z], 16)

                slots(sp, step)
                for z in range(2):
                    sp.wait_ge(s_x3_store[z], B * 8 * 16)
                    sp.wait_ge(s_n3_store[z], B * 8 * 16)

            @block.gpsimd
            def _(pool):
                g = nc.gpsimd
                n_setup = [0]

                def setup(ins, wait_for=False):
                    n_setup[0] += 1
                    ins.then_inc(s_pool_setup, 1)
                    if wait_for:
                        pool.wait_ge(s_pool_setup, n_setup[0])

                setup(g.memset(ident[:], 0.0), True)
                setup(g.affine_select(out=ident[:], in_=ident[:], compare_op=ALU.not_equal, fill=1.0, base=0,
                                      pattern=[[-1, P]], channel_multiplier=1))
                setup(g.memset(block_of[:], 1.0), True)
                setup(g.affine_select(out=block_of[:], in_=block_of[:], compare_op=ALU.is_ge, fill=0.0, base=0,
                                      pattern=[[-16, 8]], channel_multiplier=1), True)
                setup(g.affine_select(out=block_of[:], in_=block_of[:], compare_op=ALU.is_ge, fill=0.0, base=15,
                                      pattern=[[16, 8]], channel_multiplier=-1))
                setup(g.memset(decay[:], 0.9), True)
                setup(g.memset(decay[:, :, 0:1], 0.0))
                for e in range(NE):
                    setup(g.memset(first_wins[:, e:e + 1], float(NE - e)))
                setup(g.memset(minus_half[:], -0.5))
                setup(g.memset(ones3[:], 1.0), True)
                assert n_setup[0] == N_POOL_SETUP, n_setup[0]
                pool.wait_ge(s_weights, 16 * N_LOADS)
                pool.wait_ge(s_dve_setup, N_DVE_SETUP)

                def normalize(kind, src, eps_scale, eps_add, i, q, lag, reader):
                    z = par(q, lag)
                    r = rstd[kind][z]
                    ch = Chain(pool, s_pn[kind], 3, i, q, lag)
                    pool.wait_ge(s_agg[kind], at(i, q, lag))
                    wait(pool, filled[reader], at(i, q, lag + 2))
                    ch.link(g.tensor_tensor(norm[kind][z][:], src[:],
                                            mv[kind][z][:, :, 0:1].broadcast_to([P, QT, D]), ALU.subtract))
                    ch.link(g.tensor_scalar(r[:, 0, :], mv[kind][z][:, :, 1], eps_scale, eps_add, ALU.mult, ALU.add))
                    ch.join()
                    ch.link(g.tensor_tensor(r[:, 1, :], r[:, 0, :], minus_half[:], ALU.pow))
                    ch.join()
                    ch.end()
                    g.tensor_tensor(norm[kind][z][:], norm[kind][z][:],
                                    r[:, 1, :].unsqueeze(2).broadcast_to([P, QT, D]), ALU.mult).then_inc(s_norm[kind], 1)

                def second_part(kind, i, q, lag):
                    z = par(q, lag)
                    pool.wait_ge(s_hi[kind], at(i, q, lag))
                    g.tensor_tensor(split[kind][z][:, :, 1, :], norm[kind][z][:], split[kind][z][:, :, 0, :].bitcast(F32),
                                    ALU.subtract).then_inc(s_split[kind], 1)

                def step(i, q):
                    if runs(i, q, 2):
                        pool.wait_ge(s_rden, at(i, q, 2))
                        pv = probs[:].rearrange("p m t n -> p m (t n)")
                        g.tensor_tensor(pv, pv, ssum[:].unsqueeze(2).broadcast_to([P, 32, 32]),
                                        ALU.mult).then_inc(s_probs, 1)
                    if runs(i, q, 3):
                        normalize("ffn", x1[par(q, 3)], 1.0, 1e-5, i, q, 3, "ffn_t")
                        second_part("ffn", i, q, 3)
                    if runs(i, q, 1):
                        z = par(q, 1)
                        wait_apart(pool, (drained["gate"], at(i, q, 1)))
                        g.tensor_scalar(gT[z][:], gT[z][:], 1.0, None, ALU.add).then_inc(s_gp1, 1)
                    if runs(i, q, 4):
                        normalize("conv", x2[par(q, 4)], 1.0, 1e-6, i, q, 4, "conv_t")
                        second_part("conv", i, q, 4)
                        wait(pool, drained["scan_out"], at(i, q, 6))
                        z = par(q, 4)
                        g.tensor_tensor(x2_bc[z][:], x2[z][:], bcon_rows[:].unsqueeze(1).broadcast_to([P, QT, D]),
                                        ALU.add).then_inc(s_x2bc, 1)
                    if runs(i, q, 6):
                        z = par(q, 6)
                        wait(pool, s_n3_store[z], n3_stored(i, q, 8))
                        normalize("pick", x3[z], 1.0, 1e-5, i, q, 6, "pick_t")
                    if runs(i, q, 0):
                        normalize("att", x_in[q], 1.0 + 1e-5, 1e-6 * 1e-5, i, q, 0, "att_t")
                        second_part("att", i, q, 0)
                        wait(pool, drained["att_out"], at(i, q, 2))
                        g.tensor_tensor(x_bo[q][:], x_in[q][:], bo_rows[:].unsqueeze(1).broadcast_to([P, QT, D]),
                                        ALU.add).then_inc(s_bo, 1)

                slots(pool, step)

            @block.scalar
            def _(act):
                s = nc.scalar
                for k in range(2):
                    act.dma_start(wexp_raw[:, k, :], W_exp).then_inc(s_weights, 16)
                act.dma_start(wcon_raw[:], W_con.unsqueeze(1).broadcast_to([D, 2, D])).then_inc(s_weights, 16)
                act.wait_ge(s_weights, 16 * N_LOADS)
                s.mul(bgate_col[:], bgate_col[:], 0.1).then_inc(s_act_setup, 1)
                for m in range(4):
                    s.mul(w_scaled[:, m, :], w_raw[:, m, :], lnw_col[:]).then_inc(s_act_setup, 1)
                act.wait_ge(s_pe_setup, 7)
                s.copy(b_qkg[:], shared[1][:, 0:3]).then_inc(s_act_setup, 1)
                s.copy(bias_row[:, NE * D:], shared[1][0:1, P:2 * P]).then_inc(s_act_setup, 1)
                s.copy(w_expand_hi[:], shared[0][:, 0:P]).then_inc(s_act_setup, 1)
                s.mul(w_con[:], shared[0][:, P:P + D], 0.5).then_inc(s_act_setup, 1)
                s.copy(w_pick[:], shared[0][0:D, 2 * P:2 * P + EP]).then_inc(s_act_setup, 1)
                act.wait_ge(s_act_setup, 10)
                act.wait_ge(s_dve_setup, N_DVE_SETUP)

                def round_part(kind, i, q, lag, reader):
                    z = par(q, lag)
                    act.wait_ge(s_norm[kind], at(i, q, lag))
                    wait(act, filled[reader], at(i, q, lag + 2))
                    s.copy(split[kind][z][:, :, 0, :], norm[kind][z][:]).then_inc(s_hi[kind], 1)

                def step(i, q):
                    bk = lambda name: shared[bank_of(q, name)]
                    if runs(i, q, 1):
                        z = par(q, 1)
                        act.wait_ge(filled["att_t"], at(i, q, 1))
                        wait(act, s_scores, at(i, q, 3))
                        s.copy(zT[z][:], bk("att_t")[:]).then_inc(drained["att_t"], 1)
                    if runs(i, q, 3):
                        round_part("ffn", i, q, 3, "ffn_t")
                    if runs(i, q, 1):
                        act.wait_ge(filled["k"], at(i, q, 1))
                        for j in range(4):
                            ins = s.activation(kT[z][:, j, :], bk("k")[:], ACT.Identity, bias=b_k[:, j:j + 1],
                                               scale=head_of[:, j:j + 1])
                        ins.then_inc(drained["k"], 1)
                        act.wait_ge(filled["q"], at(i, q, 1))
                        s.activation(qT[z][:], bk("q")[:], ACT.Identity, bias=b_qkg[:, 0:1]).then_inc(drained["q"], 1)
                        act.wait_ge(filled["gate"], at(i, q, 1))
                        wait(act, s_og, at(i, q, 3))
                        s.activation(gT[z][:], bk("gate")[:], ACT.Tanh, bias=bg_col[:],
                                     scale=0.5).then_inc(drained["gate"], 1)
                        act.wait_ge(filled["v"], at(i, q, 1))
                        wait(act, s_o, at(i, q, 3))
                        s.copy(v_sb[z][:].rearrange("p t c -> p (t c)"), bk("v")[:]).then_inc(drained["v"], 1)
                    if runs(i, q, 3):
                        z = par(q, 3)
                        act.wait_ge(filled["ffn_t"], at(i, q, 3))
                        wait(act, filled["y3"], at(i, q, 5))
                        s.copy(tT[z][:], bk("ffn_t")[:]).then_inc(drained["ffn_t"], 1)
                    if runs(i, q, 4):
                        round_part("conv", i, q, 4, "conv_t")
                        act.wait_ge(filled["conv_t"], at(i, q, 4))
                        wait(act, filled["expand"], at(i, q, 5))
                        s.copy(cT[:], bk("conv_t")[:]).then_inc(drained["conv_t"], 1)
                    if runs(i, q, 3):
                        act.wait_ge(s_diff, at(i, q, 3))
                        s.activation(g2e[:], m2[:], ACT.Exp).then_inc(s_ratio, 1)
                    if runs(i, q, 0):
                        round_part("att", i, q, 0, "att_t")
                    if runs(i, q, 4):
                        act.wait_ge(filled["expand"], at(i, q, 4))
                        z = par(q, 4)
                        wait(act, s_gated, column(i, q, 4) * 2)
                        half = slice(z * 32, (z + 1) * 32)
                        for h in range(2):
                            rows = slice(h * D, (h + 1) * D)
                            for dst, r0, bias, scale in ((gpre, D, bgate_col, 0.1), (prim, 0, bprim_col, 1.0)):
                                src = bk("expand")[r0:r0 + D, :].rearrange("p (a h n) -> p a h n", h=2, n=8)[:, :, h, :]
                                ins = s.activation(dst[rows, :, half].rearrange("p n a -> p a n"), src, ACT.Identity,
                                                   bias=bias[r0:r0 + D], scale=scale)
                        ins.then_inc(drained["expand"], 1)
                    if runs(i, q, 1):
                        act.wait_ge(s_sub, at(i, q, 1))
                        s.activation(probs[:], probs[:], ACT.Exp, scale=float(C) ** -0.5).then_inc(s_exp, 1)
                    if runs(i, q, 6):
                        act.wait_ge(filled["pick_t"], at(i, q, 6))
                        wait(act, filled["pick"], at(i, q, 7))
                        s.copy(lT[:], bk("pick_t")[0:D, :]).then_inc(drained["pick_t"], 1)
                        z = par(q, 6)
                        act.wait_ge(filled["pick"], at(i, q, 6))
                        dst = picks[:].rearrange("p g (a b) -> p a g b", b=B)[:, z * 32:(z + 1) * 32, :, bass.ds(column(i, q, 6), 1)]
                        src = bk("pick")[:, 0:32 * NG].rearrange("p (a g) -> p a g", g=NG).unsqueeze(3)
                        s.activation(dst, src, ACT.Identity, bias=gb_col[:]).then_inc(drained["pick"], 1)
                    if q == 1 and runs(i, 1, 4):
                        act.wait_ge(s_ema, column(i, 1, 4) + 1)
                        s.activation(ema_t[:], ema[:], ACT.Tanh, scale=0.5).then_inc(s_emat, 1)

                slots(act, step)

            @block.tensor
            def _(pe):
                t_ = nc.tensor
                pe.wait_ge(s_weights, 16 * N_LOADS)
                pe.wait_ge(s_pool_setup, 2)
                t_.transpose(shared[0][:, 0:P], wexp_raw[:].rearrange("o k h -> o (k h)"), ident[:]).then_inc(s_pe_setup, 1)
                t_.transpose(shared[0][:, P:P + D], wcon_raw[:].rearrange("o k h -> o (k h)"),
                             ident[0:D, 0:D]).then_inc(s_pe_setup, 1)
                t_.transpose(shared[0][0:D, 2 * P:2 * P + EP], gw_raw[:], ident[0:EP, 0:EP]).then_inc(s_pe_setup, 1)
                for m in range(3):
                    t_.matmul(shared[1][:, m:m + 1], w_raw[0:D, m, :], lnb_col[0:D]).then_inc(s_pe_setup, 1)
                t_.matmul(shared[1][0:1, P:2 * P], lnb_col[0:D], w_raw[0:D, 3, :]).then_inc(s_pe_setup, 1)
                pe.wait_ge(s_act_setup, 10)
                pe.wait_ge(s_pool_setup, N_POOL_SETUP)
                pe.wait_ge(s_dve_setup, N_DVE_SETUP)
                pe.wait_ge(s_bias3, 16)

                def transposed(name, kind, i, q, lag):
                    for t in range(QT):
                        ins = t_.transpose(shared[bank_of(q, name)][:, t * P:(t + 1) * P],
                                           split[kind][par(q, lag)][:, t].rearrange("p k d -> p (k d)").bitcast(F32), ident[:])
                    ins.then_inc(filled[name], 1)

                def step(i, q):
                    bk = lambda name: shared[bank_of(q, name)]
                    tile = lambda t: slice(t * P, (t + 1) * P)
                    if runs(i, q, 1):
                        z = par(q, 1)
                        bank_free(pe, i, q, "att_t")
                        pe.wait_ge(s_split["att"], at(i, q, 1))
                        transposed("att_t", "att", i, q, 1)
                    if runs(i, q, 6):
                        bank_free(pe, i, q, "scan_out")
                        pe.wait_ge(s_gated, (column(i, q, 6) + 1) * 2)
                        for t in range(QT):
                            ins = t_.matmul(bk("scan_out")[:, t * D:(t + 1) * D],
                                            gated[par(q, 6)][:].rearrange("p a n -> p (a n)")[:, tile(t)], w_con[:])
                        ins.then_inc(filled["scan_out"], 1)
                    if runs(i, q, 1):
                        pe.wait_ge(drained["att_t"], at(i, q, 1))
                        for name, w in (("k", 1), ("q", 0), ("gate", 2)):
                            bank_free(pe, i, q, name)
                            t_.matmul(bk(name)[:], w_qkg_hi[:, w, :], zT[z][:], start=True, stop=False)
                            t_.matmul(bk(name)[:], w_qkg_lo[:, w, :], zT[z][:], start=False, stop=True).then_inc(filled[name], 1)
                        bank_free(pe, i, q, "v")
                        for t in range(QT):
                            t_.matmul(bk("v")[:, tile(t)], ones3[:], bias3[:, NE * D:], start=True, stop=False)
                            ins = t_.matmul(bk("v")[:, tile(t)], zT[z][:, tile(t)].bitcast(F32), w_scaled[:, 3, :],
                                            start=False, stop=True)
                        ins.then_inc(filled["v"], 1)
                    if runs(i, q, 2):
                        z2 = par(q, 2)
                        wait_apart(pe, (s_probsT, at(i, q, 2)), (drained["v"], at(i, q, 2)), (s_og, at(i, q, 3)))
                        pT = probsT[:].rearrange("p (r t h) i -> p r t h i", r=2, t=QT)
                        for t in range(QT):
                            for k in range(4):
                                for g in range(4):
                                    ins = t_.matmul(o_bank[k * 32:(k + 1) * 32, g, t * 64:(t + 1) * 64],
                                                    v_sb[z2][g * 32:(g + 1) * 32, t, k * 32:(k + 1) * 32],
                                                    pT[g * 32:(g + 1) * 32, k // 2, t, 2 * (k % 2):2 * (k % 2) + 2, :],
                                                    tile_position=(g * 32, k * 32))
                        ins.then_inc(s_o, 1)
                    if runs(i, q, 3):
                        bank_free(pe, i, q, "ffn_t")
                        pe.wait_ge(s_split["ffn"], at(i, q, 3))
                        transposed("ffn_t", "ffn", i, q, 3)
                    if runs(i, q, 4):
                        bank_free(pe, i, q, "conv_t")
                        pe.wait_ge(s_split["conv"], at(i, q, 4))
                        transposed("conv_t", "conv", i, q, 4)
                    if runs(i, q, 3):
                        z3 = par(q, 3)
                        bank_free(pe, i, q, "route")
                        pe.wait_ge(drained["ffn_t"], at(i, q, 3))
                        for t in range(QT):
                            ins = t_.matmul(bk("route")[:, t * NE:(t + 1) * NE], tT[z3][:, tile(t)].bitcast(F32), w_router[:])
                        ins.then_inc(filled["route"], 1)
                    if runs(i, q, 1):
                        wait_apart(pe, (drained["k"], at(i, q, 1)), (drained["q"], at(i, q, 1)), (s_sub, at(i, q, 2)))
                        for t in range(QT):
                            for g in range(4):
                                tok = slice(t * P + g * 32, t * P + (g + 1) * 32)
                                for r in range(2):
                                    ins = t_.matmul(s_bank[g * 32:(g + 1) * 32, r, tile(t)],
                                                    qT[z][r * 64:(r + 1) * 64, tok],
                                                    kT[z][r * 64:(r + 1) * 64, :, tok],
                                                    tile_position=(r * 64, g * 32))
                        ins.then_inc(s_scores, 1)
                    if runs(i, q, 4):
                        bank_free(pe, i, q, "expand")
                        pe.wait_ge(drained["conv_t"], at(i, q, 4))
                        t_.matmul(bk("expand")[:], w_expand_hi[:], cT[:], start=True, stop=False)
                        t_.matmul(bk("expand")[:], w_expand_lo[:], cT[:], start=False, stop=True).then_inc(filled["expand"], 1)

                    def experts(t):
                        name = f"y{t}"
                        bank_free(pe, i, q, name)
                        t_.matmul(bk(name)[:], ones3[:], bias3[:, 0:NE * D], start=True, stop=False)
                        t_.matmul(bk(name)[:], tT[z3][:, tile(t)], w_expert_hi[:], start=False, stop=False)
                        t_.matmul(bk(name)[:], tT[z3][:, tile(t)], w_expert_lo[:], start=False, stop=True).then_inc(filled[name], 1)

                    if runs(i, q, 3):
                        experts(0)
                        experts(1)
                    if runs(i, q, 2):
                        bank_free(pe, i, q, "att_out")
                        pe.wait_ge(s_og, at(i, q, 2))
                        for t in range(QT):
                            for h in range(2):
                                ins = t_.matmul(bk("att_out")[:, t * D:(t + 1) * D], ogT[:, h, tile(t)], w_o2[:, h, :],
                                                start=(h == 0), stop=(h == 1))
                        ins.then_inc(filled["att_out"], 1)
                    if runs(i, q, 3):
                        experts(2)
                        experts(3)
                    if runs(i, q, 6):
                        z6 = par(q, 6)
                        wait_apart(pe, (s_norm["pick"], at(i, q, 6)), last_drained(i, q, "pick_t"))
                        for t in range(QT):
                            ins = t_.transpose(bk("pick_t")[0:D, tile(t)], norm["pick"][z6][:, t, :], ident[:])
                        ins.then_inc(filled["pick_t"], 1)
                        wait_apart(pe, (drained["pick_t"], at(i, q, 6)), last_drained(i, q, "pick"))
                        for j in range(4):
                            mv_ = lT[:].rearrange("d (a g j) -> d a g j", g=NG, j=4)[:, :, :, j]
                            ins = t_.matmul(bk("pick")[j * EP:(j + 1) * EP, 0:32 * NG], w_pick[:], mv_,
                                            tile_position=(0, j * EP))
                        ins.then_inc(filled["pick"], 1)

                slots(pe, step)

            @block.vector
            def _(dve):
                v = nc.vector
                n_setup = [0]

                def setup(ins):
                    n_setup[0] += 1
                    ins.then_inc(s_dve_setup, 1)

                def setup_join():
                    dve.wait_ge(s_dve_setup, n_setup[0])

                dve.wait_ge(s_pool_setup, N_POOL_SETUP)
                dve.wait_ge(s_weights, 16 * N_LOADS)
                dve.wait_ge(s_act_setup, 10)
                v.memset(gated[0][:], 0.0)
                v.memset(gated[1][:], 0.0)
                v.tensor_copy(w_qkg_hi[:], w_scaled[:, 0:3, :])
                v.tensor_copy(w_expert_hi[:], w_expert[:].rearrange("d e c -> d (e c)"))
                v.tensor_copy(bias_parts[:, 0, :], bias_row[:])
                setup(v.tensor_reduce(head_of[:], block_of[:].rearrange("p (x j) -> p j x", j=4), AX.X, ALU.add))
                setup(v.tensor_reduce(odd_even[:], block_of[:].rearrange("p (x j) -> p j x", j=2), AX.X, ALU.add))
                setup_join()
                setup(v.tensor_scalar(other_big[:], odd_even[:], -BIG, BIG, ALU.mult, ALU.add))
                setup(v.tensor_tensor(w_qkg_lo[:], w_scaled[:, 0:3, :], w_qkg_hi[:].bitcast(F32), ALU.subtract))
                setup(v.tensor_tensor(w_expert_lo[:], w_expert[:].rearrange("d e c -> d (e c)"), w_expert_hi[:].bitcast(F32),
                                      ALU.subtract))
                setup(v.tensor_tensor(w_expand_lo[:], shared[0][:, 0:P], w_expand_hi[:].bitcast(F32), ALU.subtract))
                setup(v.tensor_scalar(b_k[:], head_of[:], b_qkg[:, 1:2], None, ALU.mult))
                setup(v.tensor_scalar(bg_col[:], bg_col[:], b_qkg[:, 2:3], 0.5, ALU.add, ALU.mult))
                for h in range(2):
                    setup(v.tensor_scalar(w_o2[:, h, :], w_o[:], odd_even[:, h:h + 1], 0.5, ALU.mult, ALU.mult))
                setup(v.tensor_tensor(bias_rest[:], bias_row[:], bias_parts[:, 0, :], ALU.subtract))
                setup_join()
                setup(v.tensor_copy(bias_parts[:, 1, :], bias_rest[:]))
                setup_join()
                setup(v.tensor_tensor(bias_parts[:, 2, :], bias_rest[:], bias_parts[:, 1, :], ALU.subtract))
                setup_join()
                assert n_setup[0] == N_DVE_SETUP, n_setup[0]

                def stats(kind, src, i, q, lag):
                    z = par(q, lag)
                    for t in range(QT):
                        ins = v.bn_stats(bn[kind][z][:, t, :], src[:, t, :])
                    ins.then_inc(s_bn[kind], 1)
                    wait_apart(dve, (s_bn[kind], at(i, q, lag)), (s_norm[kind], at(i, q, lag + 2)))
                    for t in range(QT):
                        ins = v.bn_aggr(mv[kind][z][:, t, :], bn[kind][z][:, t, :])
                    ins.then_inc(s_agg[kind], 1)

                def tok(ap):
                    return ap[:, 0:QT * D].rearrange("p (t d) -> p t d", d=D)

                def step(i, q):
                    bk = lambda name: shared[bank_of(q, name)]
                    if runs(i, q, 6):
                        z = par(q, 6)
                        dve.wait_ge(filled["scan_out"], at(i, q, 6))
                        dve.wait_ge(s_x2bc, at(i, q, 6))
                        wait(dve, s_x3_store[z], (column(i, q, 8) + 1) * 128)
                        wait(dve, s_norm["pick"], at(i, q, 8))
                        v.tensor_tensor(x3[z][:], tok(bk("scan_out")), x2_bc[z][:], ALU.add).then_inc(drained["scan_out"], 1)
                        dve.wait_ge(drained["scan_out"], at(i, q, 6))
                        stats("pick", x3[z], i, q, 6)
                    if runs(i, q, 4):
                        z = par(q, 4)
                        dve.wait_ge(drained["y3"], at(i, q, 4))
                        v.tensor_reduce(mixed[:].rearrange("p t d -> p (t d)"), yg[:].rearrange("p t e d -> p t d e"),
                                        AX.X, ALU.add).then_inc(s_mixed, 1)
                        dve.wait_ge(s_mixed, at(i, q, 4))
                        wait(dve, s_x2bc, at(i, q, 6))
                        v.tensor_tensor(x2[z][:], mixed[:], x1[z][:], ALU.add).then_inc(s_x2, 1)
                        dve.wait_ge(s_x2, at(i, q, 4))
                        stats("conv", x2[z], i, q, 4)
                    if runs(i, q, 2):
                        dve.wait_ge(s_probs, at(i, q, 2))
                        wait(dve, s_o, at(i, q, 3))
                        v.transpose(probsT[:].rearrange("p m i -> p (m i)"),
                                    probs[:].rearrange("p m t n -> p (m t n)")).then_inc(s_probsT, 1)
                    if runs(i, q, 0):
                        wait(dve, s_x[q], i * 128 + 128)
                        stats("att", x_in[q], i, q, 0)
                    if runs(i, q, 2):
                        z = par(q, 2)
                        dve.wait_ge(s_o, at(i, q, 2))
                        dve.wait_ge(s_gp1, at(i, q, 2))
                        wait(dve, filled["att_out"], at(i, q, 3))
                        by_group = lambda a: a.rearrange("p (t g i) -> p g t i", g=4, i=32)
                        for h in range(2):
                            o = o_bank[:, :, 0:QT * 64].rearrange("p g (t h i) -> p g t h i", h=2, i=32)[:, :, :, h, :]
                            ins = v.tensor_tensor(by_group(ogT[:, h, :]), o, by_group(gT[z][:]), ALU.mult)
                        ins.then_inc(s_og, 1)
                    if runs(i, q, 3):
                        ch = Chain(dve, s_top, 15, i, q, 3)
                        dve.wait_ge(filled["route"], at(i, q, 3))
                        v.tensor_tensor(lg[:], bk("route")[:, 0:QT * NE].rearrange("p (t e) -> p t e", e=NE),
                                        rb_rows[:].unsqueeze(1).broadcast_to([P, QT, NE]), ALU.add).then_inc(drained["route"], 1)
                        dve.wait_ge(drained["route"], at(i, q, 3))
                        wide = lambda a: a[:].unsqueeze(2).broadcast_to([P, QT, NE])

                        def best(scores, m, pick):
                            ch.link(v.tensor_reduce(m[:], scores[:], AX.X, ALU.max))
                            ch.join()
                            ch.link(v.tensor_tensor(eq[:], scores[:], wide(m), ALU.is_equal))
                            ch.join()
                            ch.link(v.tensor_tensor(eq[:], eq[:], first_wins[:].unsqueeze(1).broadcast_to([P, QT, NE]), ALU.mult))
                            ch.join()
                            ch.link(v.tensor_reduce(mw[:], eq[:], AX.X, ALU.max))
                            ch.join()
                            ch.link(v.tensor_tensor(pick[:], eq[:], wide(mw), ALU.is_equal))
                            ch.join()

                        best(lg, m1, pick1)
                        ch.link(v.scalar_tensor_tensor(lg2[:], pick1[:], -BIG, lg[:], ALU.mult, ALU.add))
                        ch.join()
                        best(lg2, m2, pick2)
                        v.tensor_tensor(m2[:], m2[:], m1[:], ALU.subtract).then_inc(s_diff, 1)
                        dve.wait_ge(s_ratio, at(i, q, 3))
                        ch.link(v.tensor_scalar(gden[:], g2e[:], 1.0, None, ALU.add))
                        ch.join()
                        ch.link(v.reciprocal(g1v[:], gden[:]))
                        ch.join()
                        ch.link(v.tensor_tensor(g2v[:], g2e[:], g1v[:], ALU.mult))
                        ch.join()
                        v.tensor_tensor(pick1[:], pick1[:], wide(g1v), ALU.mult)
                        ch.link(v.tensor_tensor(pick2[:], pick2[:], wide(g2v), ALU.mult))
                        ch.join()
                        ch.end()
                        v.tensor_tensor(gates[:], pick1[:], pick2[:], ALU.add).then_inc(s_gates, 1)
                    if runs(i, q, 1):
                        ch = Chain(dve, s_smax_chain, 3, i, q, 1)
                        dve.wait_ge(s_scores, at(i, q, 1))
                        sc = s_bank[:].rearrange("p r (m n) -> p (r m) n", n=16)
                        mx = smax[:].rearrange("p m t -> p (m t)")
                        ch.link(v.tensor_reduce(mx, sc, AX.X, ALU.max))
                        ch.join()
                        ch.link(v.tensor_tensor(smax[:], smax[:], odd_even[:].unsqueeze(1).broadcast_to([P, 32, 2]), ALU.mult))
                        ch.join()
                        ch.link(v.tensor_tensor(smax[:], smax[:], other_big[:].unsqueeze(1).broadcast_to([P, 32, 2]), ALU.add))
                        ch.join()
                        ch.end()
                        v.tensor_tensor(probs[:].rearrange("p m t n -> p (m t) n"), sc,
                                        mx.unsqueeze(2).broadcast_to([P, 64, 16]), ALU.subtract).then_inc(s_sub, 1)

                    def weigh(t):
                        dve.wait_ge(filled[f"y{t}"], at(i, q, 3))
                        if t == 0:
                            dve.wait_ge(s_gates, at(i, q, 3))
                            wait(dve, s_mixed, at(i, q, 4))
                        v.tensor_tensor(yg[:, t], bk(f"y{t}")[:].rearrange("p (e d) -> p e d", d=D),
                                        gates[:, t, :].unsqueeze(2).broadcast_to([P, NE, D]), ALU.mult).then_inc(drained[f"y{t}"], 1)

                    if runs(i, q, 3):
                        weigh(0)
                        weigh(1)
                    if runs(i, q, 2):
                        z = par(q, 2)
                        dve.wait_ge(filled["att_out"], at(i, q, 2))
                        dve.wait_ge(s_bo, at(i, q, 2))
                        wait(dve, s_norm["ffn"], at(i, q, 4))
                        wait(dve, s_x2, at(i, q, 4))
                        v.tensor_tensor(x1[z][:], tok(bk("att_out")), x_bo[z][:], ALU.add).then_inc(drained["att_out"], 1)
                        dve.wait_ge(drained["att_out"], at(i, q, 2))
                        stats("ffn", x1[z], i, q, 2)
                    if runs(i, q, 3):
                        weigh(2)
                        weigh(3)
                    if runs(i, q, 1):
                        dve.wait_ge(s_exp, at(i, q, 1))
                        v.tensor_reduce(ssum[:], probs[:].rearrange("p m t n -> p m (t n)"), AX.X, ALU.add).then_inc(s_sums, 1)
                        dve.wait_ge(s_sums, at(i, q, 1))
                        v.reciprocal(ssum[:], ssum[:]).then_inc(s_rden, 1)
                    if q == 1 and runs(i, 1, 4):
                        c = column(i, 1, 4)
                        dve.wait_ge(drained["expand"], at(i, 1, 4))
                        wait(dve, s_emat, c)
                        flat = lambda a: a[:].rearrange("p n a -> p (n a)")
                        v.tensor_tensor_scan(flat(ema), flat(decay), flat(gpre), 0.0, ALU.mult, ALU.add).then_inc(s_ema, 1)
                        dve.wait_ge(s_emat, c + 1)
                        wait(dve, filled["scan_out"], c * 2)
                        for z in range(2):
                            for h in range(2):
                                rows = slice(h * D, (h + 1) * D)
                                half = slice(z * 32, (z + 1) * 32)
                                ins = v.scalar_tensor_tensor(gated[z][rows, :, h * 8:(h + 1) * 8],
                                                             ema_t[rows, :, half].rearrange("p n a -> p a n"), 1.0,
                                                             prim[rows, :, half].rearrange("p n a -> p a n"), ALU.add, ALU.mult)
                            ins.then_inc(s_gated, 1)

                slots(dve, step)

        with ExitStack() as imgs:
            def ib(name, shape, dt=F32):
                return sb(name, shape, dt, imgs)

            w1 = ib("w1", [D + 1, EP, HID])
            w2 = ib("w2", [P, 2, EP, D])
            w2b = ib("w2b", [1, EP, D])
            ones_row = ib("ones_row", [1, N])
            best8, best8e = ib("best8", [P, 8]), ib("best8e", [P, 8])
            neg_max, psum_, prec = ib("neg_max", [P, 1]), ib("psum_", [P, 1]), ib("prec", [P, 1])
            rest = ib("rest", [P, TOK])
            wT = ib("wT", [P, IT, P])
            xi = pair("xi", [P, IT, D], F32, imgs)
            pooled = ib("pooled", [D + 1, N, EP])
            hidT = ib("hidT", [P, EP, 2, N])
            eoT = ib("eoT", [D, N, EP])
            eo = ib("eo", [P, NG, D])
            s_w = sem("w4_loaded")
            s_c = sem("c4_ready")
            s_max, s_neg, s_e, s_eb, s_rec, s_scaled, s_rep, s_wts = (sem("g_max"), sem("g_neg"), sem("g_exp"), sem("g_exp8"), sem("g_rec"),
                                                                     sem("g_scaled"), sem("g_replaced"), sem("g_weights"))
            s_wt_ps, s_wt_cp = sem("wT_filled"), sem("wT_copied")
            s_xi = [sem(f"xi_loaded{b}") for b in range(2)]
            s_xo = [sem(f"xo_stored{b}") for b in range(2)]
            s_pool_mm, s_pool_cp = sem("i_pooled"), sem("i_pooled_copied")
            banks = [s[:] for s in shared] + [s_bank[:, k] for k in range(2)] + [o_bank[:, k] for k in range(4)]
            s_hid, s_gelu, s_eo1, s_eo1c, s_eo2, s_eo2c = (sem("hid_filled"), sem("gelu_done"), sem("eoT_filled"), sem("eoT_copied"),
                                                            sem("eo_filled"), sem("eo_copied"))
            s_add_ps, s_added = sem("add_filled"), sem("added")

            block = imgs.enter_context(nc.Block())

            @block.sync
            def _(sp):
                sp.dma_start(w1[:], weight1.rearrange("e d h -> d e h")).then_inc(s_w, 16)
                for c in range(2):
                    sp.dma_start(w2[:, c], weight2[:, c * P:(c + 1) * P, :].rearrange("e h o -> h e o")).then_inc(s_w, 16)
                sp.dma_start(w2b[:], weight2[:, HID:HID + 1, :].rearrange("e one o -> one e o")).then_inc(s_w, 16)
                for n in range(N):
                    if n >= 2:
                        sp.wait_ge(s_pool_mm, n - 1)
                    sp.dma_start(xi[n % 2][:].rearrange("p t d -> p (t d)"), n3_imgs[n]).then_inc(s_xi[n % 2], 16)
                for n in range(N):
                    if n < 2:
                        sp.wait_ge(s_pool_mm, N - 1 + n)
                    else:
                        sp.wait_ge(s_xo[n % 2], 16 * (n // 2))
                    sp.dma_start(xi[n % 2][:].rearrange("p t d -> p (t d)"), x3_imgs[n]).then_inc(s_xi[n % 2], 16)
                    if n >= 1:
                        sp.wait_ge(s_added, 4 * n)
                        sp.dma_start(out_imgs[n - 1], xi[(n - 1) % 2][:].rearrange("p t d -> p (t d)")).then_inc(s_xo[(n - 1) % 2], 16)
                sp.wait_ge(s_added, 4 * N)
                sp.dma_start(out_imgs[N - 1], xi[(N - 1) % 2][:].rearrange("p t d -> p (t d)")).then_inc(s_xo[(N - 1) % 2], 16)
                for b in range(2):
                    sp.wait_ge(s_xo[b], 16 * N // 2)

            @block.gpsimd
            def _(pool):
                g = nc.gpsimd
                g.memset(ones_row[:], 1.0).then_inc(s_c, 1)
                g.memset(pooled[D:D + 1], 1.0).then_inc(s_c, 1)

            @block.scalar
            def _(act):
                s = nc.scalar
                for gr in range(NG):
                    act.wait_ge(s_neg, gr + 1)
                    s.activation(picks[:, gr, :], picks[:, gr, :], ACT.Exp, bias=neg_max[:], accum_out=psum_[:]).then_inc(s_e, 1)
                    if gr:
                        act.wait_ge(s_wts, gr)
                    s.activation(best8e[:], best8[:], ACT.Exp, bias=neg_max[:]).then_inc(s_e, 1)
                    act.wait_ge(s_rec, gr + 1)
                    s.mul(picks[:, gr, :], picks[:, gr, :], prec[:])
                    s.mul(best8e[:], best8e[:], prec[:]).then_inc(s_scaled, 1)
                    for u in range(IT // 4):
                        act.wait_ge(s_wt_ps, gr * (IT // 4) + u + 1)
                        if u == 0 and gr:
                            act.wait_ge(s_pool_mm, 4 * gr)
                        s.copy(wT[:, 4 * u:4 * u + 4, :].rearrange("p t m -> p (t m)"), banks[u % 2]).then_inc(s_wt_cp, 1)
                act.wait_ge(s_pool_mm, N)
                s.copy(pooled[0:D].rearrange("p n e -> p (n e)"), banks[2][0:D, :]).then_inc(s_pool_cp, 1)
                for u in range(2):
                    act.wait_ge(s_hid, u + 1)
                    s.activation(hidT[:, 16 * u:16 * u + 16].rearrange("p e c n -> p (e c n)"), banks[3 + u], ACT.Gelu).then_inc(s_gelu, 1)
                act.wait_ge(s_eo1, 1)
                s.copy(eoT[:].rearrange("p n e -> p e n"), banks[5][0:D, :].rearrange("p (e n) -> p e n", n=N)).then_inc(s_eo1c, 1)
                act.wait_ge(s_eo2, 1)
                s.copy(eo[:].rearrange("p g d -> p (g d)"), banks[6][:, 0:NG * D]).then_inc(s_eo2c, 1)

            @block.tensor
            def _(pe):
                t_ = nc.tensor
                pe.wait_ge(s_c, 2)
                for gr in range(NG):
                    pe.wait_ge(s_wts, gr + 1)
                    wv = picks[:, gr, :].rearrange("p (m t) -> p t m", t=IT)
                    for u in range(IT // 4):
                        if gr * (IT // 4) + u >= 2:
                            pe.wait_ge(s_wt_cp, gr * (IT // 4) + u - 1)
                        for t in range(4):
                            ins = t_.transpose(banks[u % 2][:, t * P:(t + 1) * P], wv[:, 4 * u + t, :], ident[:])
                        ins.then_inc(s_wt_ps, 1)
                    pe.wait_ge(s_wt_cp, (gr + 1) * (IT // 4))
                    for j in range(4):
                        n = 4 * gr + j
                        pe.wait_ge(s_xi[n % 2], 16 * (n // 2 + 1))
                        for t in range(IT):
                            ins = t_.matmul(banks[2][0:D, n * EP:(n + 1) * EP], xi[n % 2][:, t, :], wT[:, t, j * EP:(j + 1) * EP],
                                            start=(t == 0), stop=(t == IT - 1))
                        ins.then_inc(s_pool_mm, 1)
                pe.wait_ge(s_w, 64)
                pe.wait_ge(s_pool_cp, 1)
                for e in range(EP):
                    for c in range(2):
                        ins = t_.matmul(banks[3 + e // 16][:, ((e % 16) * 2 + c) * N:((e % 16) * 2 + c + 1) * N],
                                        w1[:, e, c * P:(c + 1) * P], pooled[:, :, e])
                    if e % 16 == 15:
                        ins.then_inc(s_hid, 1)
                for e in range(EP):
                    if e % 16 == 0:
                        pe.wait_ge(s_gelu, e // 16 + 1)
                    o = banks[5][0:D, e * N:(e + 1) * N]
                    for c in range(2):
                        t_.matmul(o, w2[:, c, e, :], hidT[:, e, c, :], start=(c == 0), stop=False)
                    ins = t_.matmul(o, w2b[:, e, :], ones_row[:], start=False, stop=True)
                ins.then_inc(s_eo1, 1)
                pe.wait_ge(s_eo1c, 1)
                for gr in range(NG):
                    ins = t_.transpose(banks[6][:, gr * D:(gr + 1) * D], eoT[:, 4 * gr:4 * gr + 4, :].rearrange("p n e -> p (n e)"),
                                       ident[0:D, 0:D])
                ins.then_inc(s_eo2, 1)
                pe.wait_ge(s_eo2c, 1)
                for n in range(N):
                    gr, j = n // 4, n % 4
                    wv = picks[:, gr, :].rearrange("p (m t) -> p t m", t=IT)
                    for u in range(4):
                        if 4 * n + u >= 8:
                            pe.wait_ge(s_added, 4 * n + u - 7)
                        for t in range(8):
                            ins = t_.matmul(banks[(4 * n + u) % 8][:, t * D:(t + 1) * D], wv[j * EP:(j + 1) * EP, 8 * u + t, :],
                                            eo[j * EP:(j + 1) * EP, gr, :], tile_position=(j * EP, 0))
                        ins.then_inc(s_add_ps, 1)

            @block.vector
            def _(dve):
                v = nc.vector
                dve.wait_ge(s_c, 2)

                for gr in range(NG):
                    v.max(best8[:], picks[:, gr, :]).then_inc(s_max, 1)
                    dve.wait_ge(s_max, gr + 1)
                    v.tensor_scalar(neg_max[:], best8[:, 0:1], -1.0, None, ALU.mult).then_inc(s_neg, 1)
                    dve.wait_ge(s_e, 2 * gr + 2)
                    v.reciprocal(prec[:], psum_[:]).then_inc(s_rec, 1)
                    dve.wait_ge(s_scaled, gr + 1)
                    v.match_replace(rest[:], best8e[:], picks[:, gr, :], 0.0).then_inc(s_rep, 1)
                    dve.wait_ge(s_rep, gr + 1)
                    v.tensor_tensor(picks[:, gr, :], picks[:, gr, :], rest[:], ALU.subtract).then_inc(s_wts, 1)
                    dve.wait_ge(s_wts, gr + 1)
                for n in range(N):
                    dve.wait_ge(s_xi[n % 2], 16 * (N // 2 + n // 2 + 1))
                    for u in range(4):
                        dve.wait_ge(s_add_ps, 4 * n + u + 1)
                        xs = xi[n % 2][:, 8 * u:8 * u + 8, :].rearrange("p t d -> p (t d)")
                        v.tensor_tensor(xs, xs, banks[(4 * n + u) % 8], ALU.add).then_inc(s_added, 1)


_INS = ['x', 'L0_conv_ln_w', 'L0_conv_ln_b', 'L0_conv_Wq', 'L0_conv_Wk', 'L0_conv_Wv', 'L0_conv_Wg', 'L0_conv_bg',
        'L0_conv_Wo', 'L0_conv_bo', 'L0_ffn_router_w', 'L0_ffn_router_b', 'L0_ffn_expert_w', 'L0_ffn_expert_b',
        'L1_conv_W_exp', 'L1_conv_b_exp', 'L1_conv_W_con', 'L1_conv_b_con', 'L1_ffn_gate_w', 'L1_ffn_gate_b',
        'L1_ffn_weight1', 'L1_ffn_weight2']


def kernel(**inputs):
    import numpy as np
    import concourse.bacc as bacc
    from concourse import mybir as mb
    from concourse.bass_utils import run_bass_kernel_spmd

    nc = bacc.Bacc("TRN2", target_bir_lowering=False, num_devices=1)
    arrays, args = {}, []
    for name in _INS:
        a = np.ascontiguousarray(inputs[name])
        arrays[f"in_{name}"] = a
        args.append(nc.dram_tensor(f"in_{name}", a.shape, mb.dt.from_np(a.dtype), kind="ExternalInput").ap())
    out = nc.dram_tensor("out_x", inputs["x"].shape, mb.dt.float32, kind="ExternalOutput").ap()
    build(nc, *args, out)
    r = run_bass_kernel_spmd(nc, [arrays], core_ids=[0])
    return r.results[0]["out_x"]
```

```python
from contextlib import ExitStack

import concourse.bass as bass
from concourse import mybir

ALU = mybir.AluOpType
ACT = mybir.ActivationFunctionType
AX = mybir.AxisListType
F32 = mybir.dt.float32
F32R = mybir.dt.float32r
BF16 = mybir.dt.bfloat16

P = 128
QT = 4
QTOK = QT * P
BIG = 1e30
NEVER, TAKEN = -3e38, -2e38

LAG = {"att_t": 1, "k": 1, "q": 1, "gate": 1, "v": 1, "scores": 2,
       "values": 3, "att_out": 3, "ffn_t": 4, "route": 4, "y0": 4, "y1": 4, "y2": 4, "y3": 4,
       "conv_t": 5, "expand": 5, "scan_out": 7, "pick_t": 8, "pick": 8, "n3_store": 8}
TURNS = ["att_t", "q", "ffn_t", "v", "scan_out", "gate", "pick", "conv_t", "y0", "expand", "y3"]
BORROWED = {"k": ("o", 0), "att_out": ("o", 1), "pick_t": ("o", 2), "route": ("o", 3),
            "y1": ("s", 0), "y2": ("s", 1)}
PEELED = 5


def build(nc, x, ln_w, ln_b, Wq, Wk, Wv, Wg, bg, Wo, bo, router_w, router_b, expert_w, expert_b,
          W_exp, b_exp, W_con, b_con, gate_w, gate_b, weight1, weight2, out):
    N, A, B, D = x.shape
    HC = Wq.shape[1]
    H = 8
    C = HC // H
    NE = router_w.shape[1]
    EP, HID = gate_w.shape[0], weight1.shape[2]
    TOK = A * B
    NG = N // 4
    IT = TOK // P
    HALVES = 2 * B
    assert HC == P and N == 16 and D == 64 and A == 64 and B == 64 and EP == 32

    def cols_of(ap):
        return ap.rearrange("n (q t p) b d -> p q b n t d", q=2, t=QT)

    def imgs_of(ap):
        return ap.rearrange("n a b d -> n (a b d)").rearrange("n (p f) -> n p f", p=P)

    x3_dram = nc.dram_tensor("x3_scratch", [N, A, B, D], F32).ap()
    n3_dram = nc.dram_tensor("normalized_x3_scratch", [N, A, B, D], F32).ap()
    x_cols, x3_cols, n3_cols = cols_of(x), cols_of(x3_dram), cols_of(n3_dram)
    x3_imgs, n3_imgs, out_imgs = imgs_of(x3_dram), imgs_of(n3_dram), imgs_of(out)

    with ExitStack() as ctx:
        def sb(name, shape, dt=F32, c=ctx):
            return c.enter_context(nc.sbuf_tensor(name, shape, dt))

        def pair(name, shape, dt=F32, c=ctx):
            return [sb(f"{name}{q}", shape, dt, c) for q in range(2)]

        def sem(name):
            return ctx.enter_context(nc.semaphore(name))

        ident = sb("ident", [P, P])
        picks = sb("picks", [P, NG, TOK])
        shared = [ctx.enter_context(nc.psum_tensor(f"shared{i}", [P, 512], F32)) for i in range(2)]
        s_bank = ctx.enter_context(nc.psum_tensor("s_bank", [P, 2, 512], F32))
        o_bank = ctx.enter_context(nc.psum_tensor("o_bank", [P, 4, 512], F32))

        with ExitStack() as cols:
            def cb(name, shape, dt=F32):
                return sb(name, shape, dt, cols)

            def cpair(name, shape, dt=F32):
                return pair(name, shape, dt, cols)

            lnw_col, lnb_col, bg_col = cb("lnw_col", [P, 1]), cb("lnb_col", [P, 1]), cb("bg_col", [P, 1])
            w_raw = cb("w_raw", [P, 4, HC])
            w_qkg_hi, w_qkg_lo = cb("w_qkg_hi", [P, 3, HC], F32R), cb("w_qkg_lo", [P, 3, HC], F32R)
            w_scaled = cb("w_scaled", [P, 4, HC])
            b_qkg = cb("b_qkg", [P, 3])
            b_k = cb("b_k", [P, H])
            w_o = cb("w_o", [P, D])
            w_o2 = cb("w_o2", [P, 2, D])
            bo_rows, bcon_rows, rb_rows = cb("bo_rows", [P, D]), cb("bcon_rows", [P, D]), cb("rb_rows", [P, NE])
            w_router = cb("w_router", [P, NE])
            w_expert = cb("w_expert", [P, NE, D])
            w_expert_hi, w_expert_lo = cb("w_expert_hi", [P, NE * D], F32R), cb("w_expert_lo", [P, NE * D], F32R)
            bias_row = cb("bias_row", [1, NE * D])
            bias_rest = cb("bias_rest", [1, NE * D])
            bias_parts = cb("bias_parts", [1, 3, NE * D], BF16)
            bias3 = cb("bias3", [3, NE * D], BF16)
            bv_terms, bv_ones = cb("bv_terms", [D, HC]), cb("bv_ones", [D, P])
            bv_rows = cb("bv_rows", [P, HC])
            ones3 = cb("ones3", [3, P], BF16)
            wexp_raw, wcon_raw, gw_raw = cb("wexp_raw", [2 * D, 2, D]), cb("wcon_raw", [D, 2, D]), cb("gw_raw", [EP, D])
            w_expand_hi, w_expand_lo = cb("w_expand_hi", [P, 2 * D], F32R), cb("w_expand_lo", [P, 2 * D], F32R)
            w_con = cb("w_con", [P, D])
            w_pick = cb("w_pick", [D, EP])
            bprim_col, bgate_col, gb_col = cb("bprim_col", [P, 1]), cb("bgate_col", [P, 1]), cb("gb_col", [P, 1])
            block_of = cb("block_of", [P, 8])
            odd_even = cb("odd_even", [P, 2])
            other_big = cb("other_big", [P, 2])
            decay = cb("decay", [P, 8, A])
            one_col = cb("one_col", [P, 1])
            minus_half = cb("minus_half", [P, QT])

            x_in = cpair("x_in", [P, QT, D])
            x_bo = cpair("x_bo", [P, QT, D])
            x1 = cpair("x1", [P, QT, D])
            x2 = cpair("x2", [P, QT, D])
            x2_bc = cpair("x2_bc", [P, QT, D])
            x3 = cpair("x3", [P, QT, D])
            KINDS = ("att", "ffn", "conv", "pick")
            norm = {k: cpair(f"norm_{k}", [P, QT, D]) for k in KINDS}
            split = {k: cpair(f"split_{k}", [P, QT, 2, D], F32R) for k in KINDS[:3]}
            bn = {k: cpair(f"bn_{k}", [P, QT, 6]) for k in KINDS}
            mv = {k: cpair(f"mv_{k}", [P, QT, 2]) for k in KINDS}
            rstd = {k: cpair(f"rstd_{k}", [P, 2, QT]) for k in KINDS}
            zT = cpair("zT", [P, QTOK], F32R)
            qT = cpair("qT", [P, QTOK])
            kT = cb("kT", [P, H, QTOK])
            gT = cpair("gT", [P, QTOK])
            v_sb = cpair("v_sb", [P, QT, HC])
            probs = cb("probs", [P, 32, 2, 16])
            probsT = cb("probsT", [P, 32, 32])
            smax = cb("smax", [P, 32, 2])
            ssum = cb("ssum", [P, 32])
            ogT = cb("ogT", [P, 2, QTOK])
            tT = cpair("tT", [P, QTOK], F32R)
            lg, marked = cb("lg", [P, QT, NE]), cb("marked", [P, QT, NE])
            top8, top2 = cb("top8", [P, QT, 8]), cb("top2", [P, QT, 8])
            lgm, lge, sel = cb("lgm", [P, QT, NE]), cb("lge", [P, QT, NE]), cb("sel", [P, QT, NE])
            gden = cb("gden", [P, QT])
            gates = cb("gates", [P, QT, NE])
            yg = cb("yg", [P, QT, NE, D])
            mixed = cb("mixed", [P, QT, D])
            cT = cb("cT", [P, QTOK], F32R)
            prim, gpre = cb("prim", [P, 8, A]), cb("gpre", [P, 8, A])
            ema, ema_t = cb("ema", [P, 8, A]), cb("ema_t", [P, 8, A])
            gated = cpair("gated", [P, A // 2, N])
            lT = cb("lT", [D, QTOK])

            s_weights, s_pool_setup, s_dve_setup = sem("weights_loaded"), sem("pool_setup"), sem("dve_setup")
            s_pe_setup, s_act_setup, s_bias3 = sem("pe_setup"), sem("act_setup"), sem("bias3_loaded")
            filled = {k: sem(f"filled_{k}") for k in TURNS + list(BORROWED)}
            drained = {k: sem(f"drained_{k}") for k in TURNS + list(BORROWED)}
            s_x = [sem(f"x_loaded{q}") for q in range(2)]
            s_bo = sem("x_bo_done")
            s_bn = {k: sem(f"stats_{k}") for k in KINDS}
            s_agg = {k: sem(f"aggregated_{k}") for k in KINDS}
            s_pn = {k: sem(f"pool_norm_{k}") for k in KINDS}
            s_norm = {k: sem(f"normalized_{k}") for k in KINDS}
            s_hi = {k: sem(f"rounded_{k}") for k in KINDS[:3]}
            s_split = {k: sem(f"split_{k}") for k in KINDS[:3]}
            s_scores, s_sub, s_exp, s_rden, s_probs, s_probsT = (sem("scores_filled"), sem("scores_read"), sem("exp_done"),
                                                                 sem("denominators"), sem("probs_normalized"), sem("probs_transposed"))
            s_smax_chain, s_o, s_og, s_gp1 = sem("softmax_chain"), sem("o_filled"), sem("o_gated"), sem("gate_plus_one")
            s_top, s_diff, s_ratio, s_gates = sem("top_chain"), sem("top_diff"), sem("top_ratio"), sem("gates_done")
            s_sums, s_v = sem("exp_summed"), sem("values_biased")
            s_mixed, s_x2, s_x2bc = sem("experts_mixed"), sem("x2_done"), sem("x2_bc_done")
            s_ema, s_emat, s_gated = sem("ema_done"), sem("ema_tanh"), sem("gated_done")
            s_x3_store = [sem(f"x3_stored{q}") for q in range(2)]
            s_n3_store = [sem(f"n3_stored{q}") for q in range(2)]

            N_LOADS = 34
            N_POOL_SETUP = 12
            N_DVE_SETUP = 12

            def at(i, q, lag, n=1, more=0):
                return i * (2 * n) + ((q - lag + 1) * n + more)

            def par(q, lag):
                return (q - lag) % 2

            def column(i, q, lag):
                return i + (q - lag - par(q, lag)) // 2

            def wait(eng, s, value):
                if not isinstance(value, int) or value > 0:
                    eng.wait_ge(s, value)

            def plain(eng):
                eng.wait_ge(s_pool_setup, N_POOL_SETUP)

            def wait_apart(eng, *waits):
                held = [(sem_, value if isinstance(value, int) else eng.to_reg(value)) for sem_, value in waits]
                plain(eng)
                for sem_, value in held:
                    wait(eng, sem_, value)

            def runs(i, q, lag):
                return not isinstance(i, int) or 0 <= 2 * i + q - lag < HALVES

            def bank_of(q, name):
                if name in BORROWED:
                    whose, bank = BORROWED[name]
                    return {"o": o_bank, "s": s_bank}[whose][:, bank]
                return shared[(len(TURNS) * q + TURNS.index(name)) % 2][:]

            def last_drained(i, q, name):
                pos = len(TURNS) * q + TURNS.index(name)
                for back in range(pos - 2, pos - 6 * len(TURNS), -2):
                    slots_back, turn = divmod(back, len(TURNS))
                    prev = TURNS[turn]
                    if not isinstance(i, int) or 0 <= 2 * i + slots_back - LAG[prev] < HALVES:
                        return drained[prev], at(i, slots_back, LAG[prev])
                return drained["pick"], 0

            def bank_free(pe, i, q, name):
                wait(pe, *last_drained(i, q, name))

            class Chain:

                def __init__(self, eng, s, per, i, q, lag):
                    self.eng, self.s, self.per, self.n = eng, s, per, 0
                    self.base = at(i, q, lag, per) - per

                def link(self, ins):
                    self.n += 1
                    ins.then_inc(self.s, 1)

                def join(self):
                    self.eng.wait_ge(self.s, self.base + self.n)

                def join_apart(self):
                    wait_apart(self.eng, (self.s, self.base + self.n))

                def end(self):
                    assert self.n == self.per, (self.n, self.per)

            def n3_stored(i, q, lag):
                return (column(i, q, lag) + 1) * 128

            def slots(engine, step):
                for i in range(PEELED):
                    for q in range(2):
                        step(i, q)
                with engine.Fori(PEELED, B) as i:
                    for q in range(2):
                        step(i, q)
                for i in range(B, B + (max(LAG.values()) + 1) // 2):
                    for q in range(2):
                        step(i, q)

            block = cols.enter_context(nc.Block())

            @block.sync
            def _(sp):
                loads = [(bg_col[:], bg.unsqueeze(1)), (w_o[:], Wo),
                         (bo_rows[:], bo.unsqueeze(0).broadcast_to([P, D])),
                         (bcon_rows[:], b_con.unsqueeze(0).broadcast_to([P, D])),
                         (rb_rows[:], router_b.unsqueeze(0).broadcast_to([P, NE])),
                         (gw_raw[:], gate_w),
                         (bias_row[:], expert_b.rearrange("e c -> (e c)").unsqueeze(0))]
                be = b_exp.rearrange("(h d) -> h d", h=2).unsqueeze(2)
                for k in range(2):
                    rows = slice(k * D, (k + 1) * D)
                    loads += [(lnw_col[rows], ln_w.unsqueeze(1)), (lnb_col[rows], ln_b.unsqueeze(1)),
                              (w_raw[rows, 0, :], Wq), (w_raw[rows, 1, :], Wk), (w_raw[rows, 2, :], Wg), (w_raw[rows, 3, :], Wv),
                              (w_router[rows], router_w), (w_expert[rows], expert_w.rearrange("e d c -> d e c")),
                              (bprim_col[rows], be[0]), (bgate_col[rows], be[1])]
                loads += [(gb_col[k * EP:(k + 1) * EP], gate_b.unsqueeze(1)) for k in range(4)]
                for dst, src in loads:
                    sp.dma_start(dst, src).then_inc(s_weights, 16)
                assert len(loads) + 3 == N_LOADS, len(loads)
                sp.wait_ge(s_dve_setup, N_DVE_SETUP)
                sp.dma_start(bias3[:], bias_parts[:]).then_inc(s_bias3, 16)

                def step(i, q):
                    if runs(i, q, 0):
                        wait(sp, s_bo, at(i, q, 2))
                        for p in range(8):
                            sp.dma_start(x_in[q][p * N:(p + 1) * N], x_cols[p, q, i]).then_inc(s_x[q], 16)
                    lag = LAG["n3_store"]
                    if runs(i, q, lag):
                        z = par(q, lag)
                        sp.wait_ge(s_norm["pick"], at(i, q, lag))
                        for p in range(8):
                            sp.dma_start(n3_cols[p, z, column(i, q, lag)],
                                         norm["pick"][z][p * N:(p + 1) * N]).then_inc(s_n3_store[z], 16)
                    lag = LAG["scan_out"]
                    if runs(i, q, lag):
                        z = par(q, lag)
                        sp.wait_ge(drained["scan_out"], at(i, q, lag))
                        for p in range(8):
                            sp.dma_start(x3_cols[p, z, column(i, q, lag)], x3[z][p * N:(p + 1) * N]).then_inc(s_x3_store[z], 16)

                slots(sp, step)
                for z in range(2):
                    sp.wait_ge(s_x3_store[z], B * 8 * 16)
                    sp.wait_ge(s_n3_store[z], B * 8 * 16)

            @block.gpsimd
            def _(pool):
                g = nc.gpsimd
                n_setup = [0]

                def setup(ins, wait_for=False):
                    n_setup[0] += 1
                    ins.then_inc(s_pool_setup, 1)
                    if wait_for:
                        pool.wait_ge(s_pool_setup, n_setup[0])

                setup(g.memset(ident[:], 0.0), True)
                setup(g.affine_select(out=ident[:], in_=ident[:], compare_op=ALU.not_equal, fill=1.0, base=0,
                                      pattern=[[-1, P]], channel_multiplier=1))
                setup(g.memset(block_of[:], 1.0), True)
                setup(g.affine_select(out=block_of[:], in_=block_of[:], compare_op=ALU.is_ge, fill=0.0, base=0,
                                      pattern=[[-16, 8]], channel_multiplier=1), True)
                setup(g.affine_select(out=block_of[:], in_=block_of[:], compare_op=ALU.is_ge, fill=0.0, base=15,
                                      pattern=[[16, 8]], channel_multiplier=-1))
                setup(g.memset(decay[:], 0.9), True)
                setup(g.memset(decay[:, :, 0:1], 0.0))
                setup(g.memset(one_col[:], 1.0))
                setup(g.memset(top2[:], NEVER))
                setup(g.memset(bv_ones[:], 1.0))
                setup(g.memset(minus_half[:], -0.5))
                setup(g.memset(ones3[:], 1.0), True)
                assert n_setup[0] == N_POOL_SETUP, n_setup[0]
                pool.wait_ge(s_weights, 16 * N_LOADS)
                pool.wait_ge(s_dve_setup, N_DVE_SETUP)

                def normalize(kind, src, eps_scale, eps_add, i, q, lag, reader):
                    z = par(q, lag)
                    r = rstd[kind][z]
                    ch = Chain(pool, s_pn[kind], 3, i, q, lag)
                    pool.wait_ge(s_agg[kind], at(i, q, lag))
                    wait(pool, filled[reader], at(i, q, lag + 2))
                    ch.link(g.tensor_tensor(norm[kind][z][:], src[:],
                                            mv[kind][z][:, :, 0:1].broadcast_to([P, QT, D]), ALU.subtract))
                    ch.link(g.tensor_scalar(r[:, 0, :], mv[kind][z][:, :, 1], eps_scale, eps_add, ALU.mult, ALU.add))
                    ch.join()
                    ch.link(g.tensor_tensor(r[:, 1, :], r[:, 0, :], minus_half[:], ALU.pow))
                    ch.join()
                    ch.end()
                    g.tensor_tensor(norm[kind][z][:], norm[kind][z][:],
                                    r[:, 1, :].unsqueeze(2).broadcast_to([P, QT, D]), ALU.mult).then_inc(s_norm[kind], 1)

                def second_part(kind, i, q, lag):
                    z = par(q, lag)
                    pool.wait_ge(s_hi[kind], at(i, q, lag))
                    g.tensor_tensor(split[kind][z][:, :, 1, :], norm[kind][z][:], split[kind][z][:, :, 0, :].bitcast(F32),
                                    ALU.subtract).then_inc(s_split[kind], 1)

                def step(i, q):
                    if runs(i, q, 4):
                        normalize("ffn", x1[par(q, 4)], 1.0, 1e-5, i, q, 4, "ffn_t")
                    if runs(i, q, 4):
                        second_part("ffn", i, q, 4)
                    if runs(i, q, 0):
                        normalize("att", x_in[q], 1.0 + 1e-5, 1e-6 * 1e-5, i, q, 0, "att_t")
                    if runs(i, q, 0):
                        second_part("att", i, q, 0)
                    if runs(i, q, 5):
                        normalize("conv", x2[par(q, 5)], 1.0, 1e-6, i, q, 5, "conv_t")
                    if runs(i, q, 1):
                        z = par(q, 1)
                        pool.wait_ge(drained["v"], at(i, q, 1))
                        g.tensor_tensor(v_sb[z][:], v_sb[z][:], bv_rows[:].unsqueeze(1).broadcast_to([P, QT, HC]),
                                        ALU.add).then_inc(s_v, 1)
                    if runs(i, q, 5):
                        second_part("conv", i, q, 5)
                    if runs(i, q, 2):
                        pool.wait_ge(s_rden, at(i, q, 2))
                        pv = probs[:].rearrange("p m t n -> p m (t n)")
                        g.tensor_tensor(pv, pv, ssum[:].unsqueeze(2).broadcast_to([P, 32, 32]),
                                        ALU.mult).then_inc(s_probs, 1)
                    if runs(i, q, 1):
                        z = par(q, 1)
                        wait(pool, drained["att_out"], at(i, q, 3))
                        g.tensor_tensor(x_bo[z][:], x_in[z][:], bo_rows[:].unsqueeze(1).broadcast_to([P, QT, D]),
                                        ALU.add).then_inc(s_bo, 1)
                    if runs(i, q, 7):
                        wait(pool, s_n3_store[par(q, 7)], n3_stored(i, q, 9))
                        normalize("pick", x3[par(q, 7)], 1.0, 1e-5, i, q, 7, "pick_t")
                    if runs(i, q, 5):
                        z = par(q, 5)
                        wait(pool, drained["scan_out"], at(i, q, 7))
                        pool.wait_ge(s_x2, at(i, q, 5))
                        g.tensor_tensor(x2_bc[z][:], x2[z][:], bcon_rows[:].unsqueeze(1).broadcast_to([P, QT, D]),
                                        ALU.add).then_inc(s_x2bc, 1)

                slots(pool, step)

            @block.scalar
            def _(act):
                s = nc.scalar
                for k in range(2):
                    act.dma_start(wexp_raw[:, k, :], W_exp).then_inc(s_weights, 16)
                act.dma_start(wcon_raw[:], W_con.unsqueeze(1).broadcast_to([D, 2, D])).then_inc(s_weights, 16)
                act.wait_ge(s_weights, 16 * N_LOADS)
                s.mul(bgate_col[:], bgate_col[:], 0.1).then_inc(s_act_setup, 1)
                for m in range(4):
                    s.mul(w_scaled[:, m, :], w_raw[:, m, :], lnw_col[:]).then_inc(s_act_setup, 1)
                s.mul(bv_terms[:], w_raw[0:D, 3, :], lnb_col[0:D]).then_inc(s_act_setup, 1)
                act.wait_ge(s_pe_setup, 7)
                s.copy(b_qkg[:], shared[1][:, 0:3]).then_inc(s_act_setup, 1)
                s.copy(bv_rows[:], shared[1][:, P:2 * P]).then_inc(s_act_setup, 1)
                s.copy(w_expand_hi[:], shared[0][:, 0:P]).then_inc(s_act_setup, 1)
                s.mul(w_con[:], shared[0][:, P:P + D], 0.5).then_inc(s_act_setup, 1)
                s.copy(w_pick[:], shared[0][0:D, 2 * P:2 * P + EP]).then_inc(s_act_setup, 1)
                act.wait_ge(s_act_setup, 11)
                act.wait_ge(s_dve_setup, N_DVE_SETUP)

                def round_part(kind, i, q, lag, reader):
                    z = par(q, lag)
                    act.wait_ge(s_norm[kind], at(i, q, lag))
                    wait(act, filled[reader], at(i, q, lag + 2))
                    s.copy(split[kind][z][:, :, 0, :], norm[kind][z][:]).then_inc(s_hi[kind], 1)

                def step(i, q):
                    bk = lambda name: bank_of(q, name)
                    z1 = par(q, 1)

                    def masked_keys(heads):
                        for h in heads:
                            ins = s.activation(kT[:, h, :], bk("k")[:], ACT.Identity, bias=b_k[:, h:h + 1],
                                               scale=block_of[:, h:h + 1])
                        return ins

                    if runs(i, q, 1):
                        act.wait_ge(filled["att_t"], at(i, q, 1))
                        wait(act, filled["k"], at(i, q, 3))
                        s.copy(zT[z1][:], bk("att_t")[:]).then_inc(drained["att_t"], 1)
                    if runs(i, q, 4):
                        round_part("ffn", i, q, 4, "ffn_t")
                    if runs(i, q, 1):
                        act.wait_ge(filled["q"], at(i, q, 1))
                        wait(act, s_scores, at(i, q, 3))
                        s.activation(qT[z1][:], bk("q")[:], ACT.Identity, bias=b_qkg[:, 0:1]).then_inc(drained["q"], 1)
                    if runs(i, q, 0):
                        round_part("att", i, q, 0, "att_t")
                    if runs(i, q, 4):
                        z = par(q, 4)
                        act.wait_ge(filled["ffn_t"], at(i, q, 4))
                        wait(act, filled["y3"], at(i, q, 6))
                        s.copy(tT[z][:], bk("ffn_t")[:]).then_inc(drained["ffn_t"], 1)
                    if runs(i, q, 1):
                        act.wait_ge(filled["v"], at(i, q, 1))
                        wait(act, s_o, at(i, q, 3))
                        s.copy(v_sb[z1][:].rearrange("p t c -> p (t c)"), bk("v")[:]).then_inc(drained["v"], 1)
                    if runs(i, q, 2):
                        act.wait_ge(s_sub, at(i, q, 2))
                        s.activation(probs[:], probs[:], ACT.Exp, scale=float(C) ** -0.5).then_inc(s_exp, 1)
                    if runs(i, q, 1):
                        act.wait_ge(filled["gate"], at(i, q, 1))
                        wait(act, s_og, at(i, q, 3))
                        s.activation(gT[z1][:], bk("gate")[:], ACT.Tanh, bias=bg_col[:],
                                     scale=0.5).then_inc(drained["gate"], 1)
                        act.wait_ge(filled["k"], at(i, q, 1))
                        wait(act, s_scores, at(i, q, 2))
                        masked_keys(range(0, 2))
                    if runs(i, q, 5):
                        round_part("conv", i, q, 5, "conv_t")
                    if runs(i, q, 8):
                        act.wait_ge(filled["pick_t"], at(i, q, 8))
                        wait(act, filled["pick"], at(i, q, 9))
                        s.copy(lT[:], bk("pick_t")[0:D, :]).then_inc(drained["pick_t"], 1)
                    if runs(i, q, 1):
                        masked_keys(range(2, 4))
                    if runs(i, q, 8):
                        z = par(q, 8)
                        act.wait_ge(filled["pick"], at(i, q, 8))
                        dst = picks[:].rearrange("p g (a b) -> p a g b", b=B)[:, z * 32:(z + 1) * 32, :, bass.ds(column(i, q, 8), 1)]
                        src = bk("pick")[:, 0:32 * NG].rearrange("p (a g) -> p a g", g=NG).unsqueeze(3)
                        s.activation(dst, src, ACT.Identity, bias=gb_col[:]).then_inc(drained["pick"], 1)
                    if runs(i, q, 5):
                        act.wait_ge(filled["conv_t"], at(i, q, 5))
                        wait(act, filled["expand"], at(i, q, 6))
                        s.copy(cT[:], bk("conv_t")[:]).then_inc(drained["conv_t"], 1)
                    if runs(i, q, 4):
                        act.wait_ge(s_diff, at(i, q, 4))
                        s.activation(lge[:], lgm[:], ACT.Exp).then_inc(s_ratio, 1)
                    if runs(i, q, 1):
                        masked_keys(range(4, 6))
                    if runs(i, q, 5):
                        z = par(q, 5)
                        act.wait_ge(filled["expand"], at(i, q, 5))
                        wait(act, s_gated, column(i, q, 5) * 2)
                        half = slice(z * 32, (z + 1) * 32)
                        for h in range(2):
                            rows = slice(h * D, (h + 1) * D)
                            for dst, r0, bias, scale in ((gpre, D, bgate_col, 0.1), (prim, 0, bprim_col, 1.0)):
                                src = bk("expand")[r0:r0 + D, :].rearrange("p (a h n) -> p a h n", h=2, n=8)[:, :, h, :]
                                ins = s.activation(dst[rows, :, half].rearrange("p n a -> p a n"), src, ACT.Identity,
                                                   bias=bias[r0:r0 + D], scale=scale)
                        ins.then_inc(drained["expand"], 1)
                    if runs(i, q, 1):
                        masked_keys(range(6, 7))
                        act.wait_ge(drained["gate"], at(i, q, 1))
                        s.activation(gT[z1][:], gT[z1][:], ACT.Identity, bias=one_col[:]).then_inc(s_gp1, 1)
                    if q == 0 and runs(i, 0, 5):
                        act.wait_ge(s_ema, column(i, 0, 5) + 1)
                        s.activation(ema_t[:], ema[:], ACT.Tanh, scale=0.5).then_inc(s_emat, 1)
                    if runs(i, q, 1):
                        masked_keys(range(7, H)).then_inc(drained["k"], 1)

                slots(act, step)

            @block.tensor
            def _(pe):
                t_ = nc.tensor
                pe.wait_ge(s_weights, 16 * N_LOADS)
                pe.wait_ge(s_pool_setup, 2)
                t_.transpose(shared[0][:, 0:P], wexp_raw[:].rearrange("o k h -> o (k h)"), ident[:]).then_inc(s_pe_setup, 1)
                t_.transpose(shared[0][:, P:P + D], wcon_raw[:].rearrange("o k h -> o (k h)"),
                             ident[0:D, 0:D]).then_inc(s_pe_setup, 1)
                t_.transpose(shared[0][0:D, 2 * P:2 * P + EP], gw_raw[:], ident[0:EP, 0:EP]).then_inc(s_pe_setup, 1)
                for m in range(3):
                    t_.matmul(shared[1][:, m:m + 1], w_raw[0:D, m, :], lnb_col[0:D]).then_inc(s_pe_setup, 1)
                pe.wait_ge(s_act_setup, 6)
                pe.wait_ge(s_pool_setup, N_POOL_SETUP)
                t_.matmul(shared[1][:, P:2 * P], bv_ones[:], bv_terms[:]).then_inc(s_pe_setup, 1)
                pe.wait_ge(s_act_setup, 11)
                pe.wait_ge(s_pool_setup, N_POOL_SETUP)
                pe.wait_ge(s_dve_setup, N_DVE_SETUP)
                pe.wait_ge(s_bias3, 16)

                def transposed(name, kind, i, q, lag):
                    for t in range(QT):
                        ins = t_.transpose(bank_of(q, name)[:, t * P:(t + 1) * P],
                                           split[kind][par(q, lag)][:, t].rearrange("p k d -> p (k d)").bitcast(F32), ident[:])
                    ins.then_inc(filled[name], 1)

                def step(i, q):
                    bk = lambda name: bank_of(q, name)
                    tile = lambda t: slice(t * P, (t + 1) * P)
                    z1, z4 = par(q, 1), par(q, 4)

                    def project(name, w):
                        if name == "k":
                            if runs(i, q, 3):
                                pe.wait_ge(s_og, at(i, q, 3))
                        else:
                            bank_free(pe, i, q, name)
                        t_.matmul(bk(name)[:], w_qkg_hi[:, w, :], zT[z1][:], start=True, stop=False)
                        t_.matmul(bk(name)[:], w_qkg_lo[:, w, :], zT[z1][:], start=False, stop=True).then_inc(filled[name], 1)

                    def experts(t):
                        y = f"y{t}"
                        if t in (1, 2):
                            pe.wait_ge(s_sub, at(i, q, 2) if runs(i, q, 2) else HALVES)
                        else:
                            bank_free(pe, i, q, y)
                        t_.matmul(bk(y)[:], ones3[:], bias3[:], start=True, stop=False)
                        t_.matmul(bk(y)[:], tT[z4][:, tile(t)], w_expert_hi[:], start=False, stop=False)
                        t_.matmul(bk(y)[:], tT[z4][:, tile(t)], w_expert_lo[:], start=False, stop=True).then_inc(filled[y], 1)

                    if runs(i, q, 1):
                        bank_free(pe, i, q, "att_t")
                        pe.wait_ge(s_split["att"], at(i, q, 1))
                        transposed("att_t", "att", i, q, 1)
                    if runs(i, q, 2):
                        z = par(q, 2)
                        wait_apart(pe, (drained["k"], at(i, q, 2)), (drained["q"], at(i, q, 2)), (s_sub, at(i, q, 3)),
                                   (drained["y2"], at(i, q, 5)))
                        for t in range(QT):
                            for g in range(4):
                                tok = slice(t * P + g * 32, t * P + (g + 1) * 32)
                                ins = t_.matmul(s_bank[g * 32:(g + 1) * 32, t // 2, (t % 2) * 256:(t % 2 + 1) * 256],
                                                qT[z][:, tok], kT[:, :, tok], tile_position=(0, g * 32))
                        ins.then_inc(s_scores, 1)
                    if runs(i, q, 1):
                        pe.wait_ge(drained["att_t"], at(i, q, 1))
                        project("q", 0)
                    if runs(i, q, 3):
                        z = par(q, 3)
                        wait_apart(pe, (s_probsT, at(i, q, 3)), (s_v, at(i, q, 3)), (s_og, at(i, q, 4)),
                                   (drained["k"], min(HALVES, at(i, q, 2)) if isinstance(i, int) else at(i, q, 2)),
                                   (drained["route"], at(i, q, 5)))
                        pT = probsT[:].rearrange("p (t m) i -> p t m i", t=QT)
                        for t in range(QT):
                            for k in range(4):
                                for g in range(4):
                                    ins = t_.matmul(o_bank[k * 32:(k + 1) * 32, g, t * 64:(t + 1) * 64],
                                                    v_sb[z][g * 32:(g + 1) * 32, t, k * 32:(k + 1) * 32],
                                                    pT[g * 32:(g + 1) * 32, t, 2 * k:2 * k + 2, :],
                                                    tile_position=(g * 32, k * 32))
                        ins.then_inc(s_o, 1)
                    if runs(i, q, 4):
                        bank_free(pe, i, q, "ffn_t")
                        pe.wait_ge(s_split["ffn"], at(i, q, 4))
                        transposed("ffn_t", "ffn", i, q, 4)
                    if runs(i, q, 1):
                        bank_free(pe, i, q, "v")
                        for t in range(QT):
                            ins = t_.matmul(bk("v")[:, tile(t)], zT[z1][:, tile(t)].bitcast(F32), w_scaled[:, 3, :])
                        ins.then_inc(filled["v"], 1)
                    if runs(i, q, 7):
                        bank_free(pe, i, q, "scan_out")
                        pe.wait_ge(s_gated, at(i, q, 7))
                        for t in range(QT):
                            ins = t_.matmul(bk("scan_out")[:, t * D:(t + 1) * D],
                                            gated[par(q, 7)][:].rearrange("p a n -> p (a n)")[:, tile(t)], w_con[:])
                        ins.then_inc(filled["scan_out"], 1)
                    if runs(i, q, 1):
                        project("gate", 2)
                        project("k", 1)
                    if runs(i, q, 3):
                        pe.wait_ge(s_og, at(i, q, 3))
                        for t in range(QT):
                            for h in range(2):
                                ins = t_.matmul(bk("att_out")[:, t * D:(t + 1) * D], ogT[:, h, tile(t)], w_o2[:, h, :],
                                                start=(h == 0), stop=(h == 1))
                        ins.then_inc(filled["att_out"], 1)
                    if runs(i, q, 8):
                        wait_apart(pe, (s_norm["pick"], at(i, q, 8)))
                        for t in range(QT):
                            ins = t_.transpose(bk("pick_t")[0:D, tile(t)], norm["pick"][par(q, 8)][:, t, :], ident[:])
                        ins.then_inc(filled["pick_t"], 1)
                    if runs(i, q, 4):
                        pe.wait_ge(drained["ffn_t"], at(i, q, 4))
                        for t in range(QT):
                            ins = t_.matmul(bk("route")[:, t * NE:(t + 1) * NE], tT[z4][:, tile(t)].bitcast(F32), w_router[:])
                        ins.then_inc(filled["route"], 1)
                    if runs(i, q, 8):
                        wait_apart(pe, (drained["pick_t"], at(i, q, 8)), last_drained(i, q, "pick"))
                        for j in range(4):
                            mv_ = lT[:].rearrange("d (a g j) -> d a g j", g=NG, j=4)[:, :, :, j]
                            ins = t_.matmul(bk("pick")[j * EP:(j + 1) * EP, 0:32 * NG], w_pick[:], mv_,
                                            tile_position=(0, j * EP))
                        ins.then_inc(filled["pick"], 1)
                    if runs(i, q, 5):
                        bank_free(pe, i, q, "conv_t")
                        pe.wait_ge(s_split["conv"], at(i, q, 5))
                        transposed("conv_t", "conv", i, q, 5)
                    if runs(i, q, 4):
                        experts(0)
                    if runs(i, q, 5):
                        bank_free(pe, i, q, "expand")
                        pe.wait_ge(drained["conv_t"], at(i, q, 5))
                        t_.matmul(bk("expand")[:], w_expand_hi[:], cT[:], start=True, stop=False)
                        t_.matmul(bk("expand")[:], w_expand_lo[:], cT[:], start=False, stop=True).then_inc(filled["expand"], 1)
                    if runs(i, q, 4):
                        for t in range(1, QT):
                            experts(t)

                slots(pe, step)

            @block.vector
            def _(dve):
                v = nc.vector
                n_setup = [0]

                def setup(ins):
                    n_setup[0] += 1
                    ins.then_inc(s_dve_setup, 1)

                def setup_join():
                    dve.wait_ge(s_dve_setup, n_setup[0])

                dve.wait_ge(s_pool_setup, N_POOL_SETUP)
                dve.wait_ge(s_weights, 16 * N_LOADS)
                dve.wait_ge(s_act_setup, 11)
                v.memset(gated[0][:], 0.0)
                v.memset(gated[1][:], 0.0)
                v.tensor_copy(w_qkg_hi[:], w_scaled[:, 0:3, :])
                v.tensor_copy(w_expert_hi[:], w_expert[:].rearrange("d e c -> d (e c)"))
                v.tensor_copy(bias_parts[:, 0, :], bias_row[:])
                setup(v.tensor_reduce(odd_even[:], block_of[:].rearrange("p (x j) -> p j x", j=2), AX.X, ALU.add))
                setup_join()
                setup(v.tensor_scalar(other_big[:], odd_even[:], -BIG, BIG, ALU.mult, ALU.add))
                setup(v.tensor_tensor(w_qkg_lo[:], w_scaled[:, 0:3, :], w_qkg_hi[:].bitcast(F32), ALU.subtract))
                setup(v.tensor_tensor(w_expert_lo[:], w_expert[:].rearrange("d e c -> d (e c)"), w_expert_hi[:].bitcast(F32),
                                      ALU.subtract))
                setup(v.tensor_tensor(w_expand_lo[:], shared[0][:, 0:P], w_expand_hi[:].bitcast(F32), ALU.subtract))
                setup(v.tensor_scalar(b_k[:], block_of[:], b_qkg[:, 1:2], None, ALU.mult))
                setup(v.tensor_scalar(bg_col[:], bg_col[:], b_qkg[:, 2:3], 0.5, ALU.add, ALU.mult))
                for h in range(2):
                    setup(v.tensor_scalar(w_o2[:, h, :], w_o[:], odd_even[:, h:h + 1], 0.5, ALU.mult, ALU.mult))
                setup(v.tensor_tensor(bias_rest[:], bias_row[:], bias_parts[:, 0, :], ALU.subtract))
                setup_join()
                setup(v.tensor_copy(bias_parts[:, 1, :], bias_rest[:]))
                setup_join()
                setup(v.tensor_tensor(bias_parts[:, 2, :], bias_rest[:], bias_parts[:, 1, :], ALU.subtract))
                setup_join()
                assert n_setup[0] == N_DVE_SETUP, n_setup[0]

                def stats(kind, src, i, q, lag):
                    z = par(q, lag)
                    for t in range(QT):
                        ins = v.bn_stats(bn[kind][z][:, t, :], src[:, t, :])
                    ins.then_inc(s_bn[kind], 1)
                    wait_apart(dve, (s_bn[kind], at(i, q, lag)), (s_norm[kind], at(i, q, lag + 2)))
                    for t in range(QT):
                        ins = v.bn_aggr(mv[kind][z][:, t, :], bn[kind][z][:, t, :])
                    ins.then_inc(s_agg[kind], 1)

                def tok(ap):
                    return ap[:, 0:QT * D].rearrange("p (t d) -> p t d", d=D)

                def step(i, q):
                    bk = lambda name: bank_of(q, name)

                    def gate_primary():
                        c = column(i, q, 5 + q)
                        dve.wait_ge(s_emat, c + 1)
                        wait(dve, filled["scan_out"], c * 2)
                        half = slice(q * 32, (q + 1) * 32)
                        for h in range(2):
                            rows = slice(h * D, (h + 1) * D)
                            ins = v.scalar_tensor_tensor(gated[q][rows, :, h * 8:(h + 1) * 8],
                                                         ema_t[rows, :, half].rearrange("p n a -> p a n"), 1.0,
                                                         prim[rows, :, half].rearrange("p n a -> p a n"), ALU.add, ALU.mult)
                        ins.then_inc(s_gated, 1)

                    if runs(i, q, 0):
                        wait(dve, s_x[q], i * 128 + 128)
                        stats("att", x_in[q], i, q, 0)
                    if runs(i, q, 5):
                        z = par(q, 5)
                        dve.wait_ge(drained["y3"], at(i, q, 5))
                        v.tensor_reduce(mixed[:].rearrange("p t d -> p (t d)"), yg[:].rearrange("p t e d -> p t d e"),
                                        AX.X, ALU.add).then_inc(s_mixed, 1)
                    if runs(i, q, 2):
                        ch = Chain(dve, s_smax_chain, 3, i, q, 2)
                        dve.wait_ge(s_scores, at(i, q, 2))
                        sc = s_bank[:].rearrange("p r (m n) -> p (r m) n", n=16)
                        mx = smax[:].rearrange("p m t -> p (m t)")
                        ch.link(v.tensor_reduce(mx, sc, AX.X, ALU.max))
                        ch.join()
                        ch.link(v.tensor_tensor(smax[:], smax[:], odd_even[:].unsqueeze(1).broadcast_to([P, 32, 2]), ALU.mult))
                        ch.join()
                        ch.link(v.tensor_tensor(smax[:], smax[:], other_big[:].unsqueeze(1).broadcast_to([P, 32, 2]), ALU.add))
                        ch.join()
                        ch.end()
                        v.tensor_tensor(probs[:].rearrange("p m t n -> p (m t) n"), sc,
                                        mx.unsqueeze(2).broadcast_to([P, 64, 16]), ALU.subtract).then_inc(s_sub, 1)
                    if runs(i, q, 5):
                        z = par(q, 5)
                        dve.wait_ge(s_mixed, at(i, q, 5))
                        wait(dve, s_x2bc, at(i, q, 7))
                        v.tensor_tensor(x2[z][:], mixed[:], x1[z][:], ALU.add).then_inc(s_x2, 1)
                        dve.wait_ge(s_x2, at(i, q, 5))
                        stats("conv", x2[z], i, q, 5)
                    if runs(i, q, 3):
                        z = par(q, 3)
                        dve.wait_ge(s_o, at(i, q, 3))
                        dve.wait_ge(s_gp1, at(i, q, 3))
                        wait(dve, filled["att_out"], at(i, q, 4))
                        by_group = lambda a: a.rearrange("p (t g i) -> p g t i", g=4, i=32)
                        for h in range(2):
                            o = o_bank[:, :, 0:QT * 64].rearrange("p g (t h i) -> p g t h i", h=2, i=32)[:, :, :, h, :]
                            ins = v.tensor_tensor(by_group(ogT[:, h, :]), o, by_group(gT[z][:]), ALU.mult)
                        ins.then_inc(s_og, 1)
                    if runs(i, q, 7):
                        z = par(q, 7)
                        dve.wait_ge(filled["scan_out"], at(i, q, 7))
                        dve.wait_ge(s_x2bc, at(i, q, 7))
                        wait(dve, s_x3_store[z], (column(i, q, 9) + 1) * 128)
                        wait(dve, s_norm["pick"], at(i, q, 9))
                        v.tensor_tensor(x3[z][:], tok(bk("scan_out")), x2_bc[z][:], ALU.add).then_inc(drained["scan_out"], 1)
                    if runs(i, q, 2):
                        dve.wait_ge(s_exp, at(i, q, 2))
                        v.tensor_reduce(ssum[:], probs[:].rearrange("p m t n -> p m (t n)"), AX.X, ALU.add).then_inc(s_sums, 1)
                        dve.wait_ge(s_sums, at(i, q, 2))
                        v.reciprocal(ssum[:], ssum[:]).then_inc(s_rden, 1)
                    if q == 1 and runs(i, 1, 6):
                        gate_primary()
                    if runs(i, q, 3):
                        z = par(q, 3)
                        dve.wait_ge(filled["att_out"], at(i, q, 3))
                        dve.wait_ge(s_bo, at(i, q, 3))
                        wait(dve, s_norm["ffn"], at(i, q, 5))
                        wait(dve, s_x2, at(i, q, 5))
                        v.tensor_tensor(x1[z][:], tok(bk("att_out")), x_bo[z][:], ALU.add).then_inc(drained["att_out"], 1)
                        dve.wait_ge(drained["att_out"], at(i, q, 3))
                        stats("ffn", x1[z], i, q, 3)
                    if runs(i, q, 7):
                        dve.wait_ge(drained["scan_out"], at(i, q, 7))
                        stats("pick", x3[par(q, 7)], i, q, 7)
                    if runs(i, q, 4):
                        ch = Chain(dve, s_top, 6, i, q, 4)
                        wide = lambda a: a.broadcast_to([P, QT, NE])
                        dve.wait_ge(filled["route"], at(i, q, 4))
                        v.tensor_tensor(lg[:], bk("route")[:, 0:QT * NE].rearrange("p (t e) -> p t e", e=NE),
                                        rb_rows[:].unsqueeze(1).broadcast_to([P, QT, NE]), ALU.add).then_inc(drained["route"], 1)
                        wait_apart(dve, (drained["route"], at(i, q, 4)))
                        for t in range(QT):
                            ins = v.max(top8[:, t, :], lg[:, t, :])
                        ch.link(ins)
                        ch.join()
                        ch.link(v.tensor_copy(top2[:, :, 0:2], top8[:, :, 0:2]))
                        v.tensor_tensor(lgm[:], lg[:], wide(top8[:, :, 0:1]), ALU.subtract).then_inc(s_diff, 1)
                        ch.join_apart()
                        for t in range(QT):
                            ins = v.match_replace(marked[:, t, :], top2[:, t, :], lg[:, t, :], TAKEN)
                        ch.link(ins)
                        ch.join()
                        dve.wait_ge(s_ratio, at(i, q, 4))
                        ch.link(v.scalar_tensor_tensor(sel[:], marked[:], TAKEN, lge[:], ALU.is_equal, ALU.mult))
                        ch.join()
                        ch.link(v.tensor_reduce(gden[:], sel[:], AX.X, ALU.add))
                        ch.join()
                        ch.link(v.reciprocal(gden[:], gden[:]))
                        ch.join()
                        ch.end()
                        v.tensor_tensor(gates[:], sel[:], wide(gden[:].unsqueeze(2)), ALU.mult).then_inc(s_gates, 1)
                    if runs(i, q, 4):
                        dve.wait_ge(s_gates, at(i, q, 4))
                        wait(dve, s_mixed, at(i, q, 5))
                        for t in range(2):
                            y = f"y{t}"
                            dve.wait_ge(filled[y], at(i, q, 4))
                            v.tensor_tensor(yg[:, t], bk(y)[:].rearrange("p (e d) -> p e d", d=D),
                                            gates[:, t, :].unsqueeze(2).broadcast_to([P, NE, D]), ALU.mult).then_inc(drained[y], 1)
                    if runs(i, q, 2):
                        dve.wait_ge(s_probs, at(i, q, 2))
                        wait(dve, s_o, at(i, q, 3))
                        v.transpose(probsT[:].rearrange("p m i -> p (m i)"),
                                    probs[:].rearrange("p m t n -> p (m t n)")).then_inc(s_probsT, 1)
                    if q == 0 and runs(i, 0, 5):
                        c = column(i, 0, 5)
                        dve.wait_ge(drained["expand"], at(i, 0, 5))
                        wait(dve, s_emat, c)
                        flat = lambda a: a[:].rearrange("p n a -> p (n a)")
                        v.tensor_tensor_scan(flat(ema), flat(decay), flat(gpre), 0.0, ALU.mult, ALU.add).then_inc(s_ema, 1)
                    if runs(i, q, 4):
                        for t in range(2, QT):
                            y = f"y{t}"
                            dve.wait_ge(filled[y], at(i, q, 4))
                            v.tensor_tensor(yg[:, t], bk(y)[:].rearrange("p (e d) -> p e d", d=D),
                                            gates[:, t, :].unsqueeze(2).broadcast_to([P, NE, D]), ALU.mult).then_inc(drained[y], 1)
                    if q == 0 and runs(i, 0, 5):
                        gate_primary()

                slots(dve, step)

        banks = [s[:] for s in shared] + [s_bank[:, k] for k in range(2)] + [o_bank[:, k] for k in range(4)]
        with ExitStack() as imgs:
            xa = sb("xa", [P, 4, IT, D], F32, imgs)
            eo = sb("eo", [P, NG, 4, D], F32, imgs)
            s_x4 = [sem(f"x4_loaded{b}") for b in range(2)]

            with ExitStack() as pooling:
                def ib(name, shape, dt=F32):
                    return sb(name, shape, dt, pooling)

                w1 = ib("w1", [D + 1, EP, HID])
                w2 = ib("w2", [P, 2, EP, D])
                w2b = ib("w2b", [1, EP, D])
                ones_row = ib("ones_row", [1, N])
                best8, best8e = ib("best8", [P, NG, 8]), ib("best8e", [P, NG, 8])
                neg_max, psum_, prec = ib("neg_max", [P, NG]), ib("psum_", [P, NG]), ib("prec", [P, NG])
                rest = ib("rest", [P, TOK])
                wT = ib("wT", [P, IT, P])
                pooled = ib("pooled", [D + 1, N, EP])
                hidT = ib("hidT", [P, EP, 2, N])
                eoT = ib("eoT", [D, N, EP])
                s_w, s_c = sem("w4_loaded"), sem("c4_ready")
                s_max, s_neg, s_e = sem("g_max"), sem("g_neg"), sem("g_exp")
                s_rep, s_kept, s_wts = sem("g_replaced"), sem("g_kept"), sem("g_weights")
                s_wt_ps, s_wt_cp = sem("wT_filled"), sem("wT_copied")
                s_xi = [sem(f"xi_loaded{b}") for b in range(4)]
                s_pool_mm, s_pool_cp = sem("pair_pooled"), sem("pooled_copied")
                s_hid, s_gelu, s_eo1, s_eo1c, s_eo2, s_eo2c = (sem("hid_filled"), sem("gelu_done"), sem("eoT_filled"),
                                                                sem("eoT_copied"), sem("eo_filled"), sem("eo_copied"))
                block = pooling.enter_context(nc.Block())

                @block.sync
                def _(sp):
                    sp.dma_start(w1[:], weight1.rearrange("e d h -> d e h")).then_inc(s_w, 16)
                    for c in range(2):
                        sp.dma_start(w2[:, c], weight2[:, c * P:(c + 1) * P, :].rearrange("e h o -> h e o")).then_inc(s_w, 16)
                    sp.dma_start(w2b[:], weight2[:, HID:HID + 1, :].rearrange("e one o -> one e o")).then_inc(s_w, 16)
                    for n in range(N):
                        if n >= 4:
                            sp.wait_ge(s_pool_mm, (n - 4) // 2 + 1)
                        sp.dma_start(xa[:, n % 4].rearrange("p t d -> p (t d)"), n3_imgs[n]).then_inc(s_xi[n % 4], 16)
                    for j in range(4):
                        sp.wait_ge(s_pool_mm, (N - 4 + j) // 2 + 1)
                        sp.dma_start(xa[:, j].rearrange("p t d -> p (t d)"), x3_imgs[j]).then_inc(s_x4[0], 16)

                @block.gpsimd
                def _(pool):
                    g = nc.gpsimd
                    g.memset(ones_row[:], 1.0).then_inc(s_c, 1)
                    pool.wait_ge(s_c, 1)
                    g.memset(pooled[D:D + 1], 1.0).then_inc(s_c, 1)
                    pool.wait_ge(s_c, 2)
                    g.memset(eo[:], 0.0).then_inc(s_c, 1)

                @block.scalar
                def _(act):
                    s = nc.scalar

                    def exps(gr):
                        act.wait_ge(s_neg, gr + 1)
                        bias = neg_max[:, gr:gr + 1]
                        s.activation(picks[:, gr, :], picks[:, gr, :], ACT.Exp, bias=bias, accum_out=psum_[:, gr:gr + 1]).then_inc(s_e, 1)
                        s.activation(best8e[:, gr, :], best8[:, gr, :], ACT.Exp, bias=bias).then_inc(s_e, 1)

                    act.wait_ge(s_c, 3)
                    exps(0)
                    for gr in range(NG):
                        if gr + 1 < NG:
                            exps(gr + 1)
                        act.wait_ge(s_kept, gr + 1)
                        s.mul(picks[:, gr, :], picks[:, gr, :], prec[:, gr:gr + 1]).then_inc(s_wts, 1)
                        for u in range(IT // 4):
                            act.wait_ge(s_wt_ps, gr * (IT // 4) + u + 1)
                            if u == 0 and gr:
                                act.wait_ge(s_pool_mm, 2 * gr)
                            s.copy(wT[:, 4 * u:4 * u + 4, :].rearrange("p t m -> p (t m)"), banks[u % 2]).then_inc(s_wt_cp, 1)
                    act.wait_ge(s_pool_mm, N // 2)
                    for b in range(2):
                        ins = s.copy(pooled[0:D].rearrange("p (m b) e -> p b m e", b=2)[:, b],
                                     banks[2][b * D:(b + 1) * D, 0:N // 2 * EP].rearrange("p (m e) -> p m e", e=EP))
                    ins.then_inc(s_pool_cp, 1)
                    for u in range(2):
                        act.wait_ge(s_hid, u + 1)
                        s.activation(hidT[:, 16 * u:16 * u + 16].rearrange("p e c n -> p (e c n)"), banks[3 + u], ACT.Gelu).then_inc(s_gelu, 1)
                    act.wait_ge(s_eo1, 1)
                    s.copy(eoT[:].rearrange("p n e -> p e n"), banks[5][0:D, :].rearrange("p (e n) -> p e n", n=N)).then_inc(s_eo1c, 1)
                    act.wait_ge(s_eo2, 1)
                    for j in range(4):
                        rows = slice(j * EP, (j + 1) * EP)
                        s.copy(eo[rows, :, j, :], banks[6][rows, 0:NG * D].rearrange("p (g d) -> p g d", g=NG)).then_inc(s_eo2c, 1)

                @block.tensor
                def _(pe):
                    t_ = nc.tensor
                    pe.wait_ge(s_c, 3)
                    for gr in range(NG):
                        pe.wait_ge(s_wts, gr + 1)
                        wv = picks[:, gr, :].rearrange("p (m t) -> p t m", t=IT)
                        for u in range(IT // 4):
                            if gr * (IT // 4) + u >= 2:
                                pe.wait_ge(s_wt_cp, gr * (IT // 4) + u - 1)
                            for t in range(4):
                                ins = t_.transpose(banks[u % 2][:, t * P:(t + 1) * P], wv[:, 4 * u + t, :], ident[:])
                            ins.then_inc(s_wt_ps, 1)
                        pe.wait_ge(s_wt_cp, (gr + 1) * (IT // 4))
                        for pr in range(2):
                            m = 2 * gr + pr
                            for b in range(2):
                                pe.wait_ge(s_xi[2 * pr + b], 16 * (gr + 1))
                            for t in range(IT):
                                for b in range(2):
                                    j = 2 * pr + b
                                    ins = t_.matmul(banks[2][b * D:(b + 1) * D, m * EP:(m + 1) * EP], xa[:, j, t, :],
                                                    wT[:, t, j * EP:(j + 1) * EP], start=(t == 0), stop=(t == IT - 1),
                                                    tile_position=(0, b * D))
                            ins.then_inc(s_pool_mm, 1)
                    pe.wait_ge(s_w, 64)
                    pe.wait_ge(s_pool_cp, 1)
                    for e in range(EP):
                        for c in range(2):
                            ins = t_.matmul(banks[3 + e // 16][:, ((e % 16) * 2 + c) * N:((e % 16) * 2 + c + 1) * N],
                                            w1[:, e, c * P:(c + 1) * P], pooled[:, :, e])
                        if e % 16 == 15:
                            ins.then_inc(s_hid, 1)
                    for e in range(EP):
                        if e % 16 == 0:
                            pe.wait_ge(s_gelu, e // 16 + 1)
                        o = banks[5][0:D, e * N:(e + 1) * N]
                        for c in range(2):
                            t_.matmul(o, w2[:, c, e, :], hidT[:, e, c, :], start=(c == 0), stop=False)
                        ins = t_.matmul(o, w2b[:, e, :], ones_row[:], start=False, stop=True)
                    ins.then_inc(s_eo1, 1)
                    pe.wait_ge(s_eo1c, 1)
                    for gr in range(NG):
                        ins = t_.transpose(banks[6][:, gr * D:(gr + 1) * D], eoT[:, 4 * gr:4 * gr + 4, :].rearrange("p n e -> p (n e)"),
                                           ident[0:D, 0:D])
                    ins.then_inc(s_eo2, 1)

                @block.vector
                def _(dve):
                    v = nc.vector

                    def best(gr):
                        v.max(best8[:, gr, :], picks[:, gr, :]).then_inc(s_max, 1)
                        dve.wait_ge(s_max, gr + 1)
                        v.tensor_scalar(neg_max[:, gr:gr + 1], best8[:, gr, 0:1], -1.0, None, ALU.mult).then_inc(s_neg, 1)

                    best(0)
                    for gr in range(NG):
                        if gr + 1 < NG:
                            best(gr + 1)
                        dve.wait_ge(s_e, 2 * gr + 2)
                        v.reciprocal(prec[:, gr:gr + 1], psum_[:, gr:gr + 1])
                        v.match_replace(rest[:], best8e[:, gr, :], picks[:, gr, :], 0.0).then_inc(s_rep, 1)
                        dve.wait_ge(s_rep, gr + 1)
                        v.tensor_tensor(picks[:, gr, :], picks[:, gr, :], rest[:], ALU.subtract).then_inc(s_kept, 1)
                        dve.wait_ge(s_kept, gr + 1)

            with ExitStack() as adding:
                xb = sb("xb", [P, 4, IT, D], F32, adding)
                quads = [xa, xb]
                UNITS = IT // 2
                s_xo = [sem(f"xo_stored{b}") for b in range(2)]
                s_add_ps, s_added = sem("add_filled"), sem("added")
                block = adding.enter_context(nc.Block())

                @block.scalar
                def _(act):
                    for gr in range(1, NG):
                        if gr >= 2:
                            act.wait_ge(s_xo[gr % 2], 128 * (gr // 2))
                        for j in range(4):
                            act.dma_start(quads[gr % 2][:, j].rearrange("p t d -> p (t d)"),
                                          x3_imgs[4 * gr + j]).then_inc(s_x4[gr % 2], 16)

                @block.sync
                def _(sp):
                    for gr in range(NG):
                        for half in range(2):
                            sp.wait_ge(s_added, UNITS * gr + (half + 1) * UNITS // 2)
                            tiles = slice(half * IT // 2, (half + 1) * IT // 2)
                            for j in range(4):
                                sp.dma_start(out_imgs[4 * gr + j].rearrange("p (t d) -> p t d", d=D)[:, tiles],
                                             quads[gr % 2][:, j, tiles]).then_inc(s_xo[gr % 2], 16)
                    for b in range(2):
                        sp.wait_ge(s_xo[b], 128 * NG // 2)

                @block.tensor
                def _(pe):
                    for gr in range(NG):
                        wv = picks[:, gr, :].rearrange("p (m t) -> p t m", t=IT)
                        for u in range(UNITS):
                            k = UNITS * gr + u
                            if k >= 8:
                                pe.wait_ge(s_added, k - 7)
                            for t in range(2):
                                ins = nc.tensor.matmul(banks[k % 8][:, t * 4 * D:(t + 1) * 4 * D], wv[:, 2 * u + t, :],
                                                       eo[:, gr].rearrange("p j d -> p (j d)"))
                            ins.then_inc(s_add_ps, 1)

                @block.vector
                def _(dve):
                    for gr in range(NG):
                        dve.wait_ge(s_x4[gr % 2], 64 * (gr // 2 + 1))
                        for u in range(UNITS):
                            k = UNITS * gr + u
                            dve.wait_ge(s_add_ps, k + 1)
                            xs = quads[gr % 2][:, :, 2 * u:2 * u + 2, :]
                            nc.vector.tensor_tensor(xs, xs, banks[k % 8].rearrange("p (t j d) -> p j t d", t=2, j=4),
                                                    ALU.add).then_inc(s_added, 1)


_INS = ['x', 'L0_conv_ln_w', 'L0_conv_ln_b', 'L0_conv_Wq', 'L0_conv_Wk', 'L0_conv_Wv', 'L0_conv_Wg', 'L0_conv_bg',
        'L0_conv_Wo', 'L0_conv_bo', 'L0_ffn_router_w', 'L0_ffn_router_b', 'L0_ffn_expert_w', 'L0_ffn_expert_b',
        'L1_conv_W_exp', 'L1_conv_b_exp', 'L1_conv_W_con', 'L1_conv_b_con', 'L1_ffn_gate_w', 'L1_ffn_gate_b',
        'L1_ffn_weight1', 'L1_ffn_weight2']


def kernel(**inputs):
    import numpy as np
    import concourse.bacc as bacc
    from concourse import mybir as mb
    from concourse.bass_utils import run_bass_kernel_spmd

    nc = bacc.Bacc("TRN2", target_bir_lowering=False, num_devices=1)
    arrays, args = {}, []
    for name in _INS:
        a = np.ascontiguousarray(inputs[name])
        arrays[f"in_{name}"] = a
        args.append(nc.dram_tensor(f"in_{name}", a.shape, mb.dt.from_np(a.dtype), kind="ExternalInput").ap())
    out = nc.dram_tensor("out_x", inputs["x"].shape, mb.dt.float32, kind="ExternalOutput").ap()
    build(nc, *args, out)
    r = run_bass_kernel_spmd(nc, [arrays], core_ids=[0])
    return r.results[0]["out_x"]
```
